# Optimizing a Trainium2 kernel written in Bass

```python
import numpy as np
import jax
import jax.numpy as jnp

def _softmax(x, axis=-1):
    return jax.nn.softmax(x, axis=axis)

def _gelu(x):
    return jax.nn.gelu(x, approximate=True)

def _silu(x):
    return jax.nn.silu(x)

def _sigmoid(x):
    return jax.nn.sigmoid(x)

def _layernorm(x, axis=-1, eps=1e-05):
    m = jnp.mean(x, axis=axis, keepdims=True)
    v = jnp.var(x, axis=axis, keepdims=True)
    return (x - m) / jnp.sqrt(v + eps)

def _scatter_add(tgt, idx, src, axis=0):
    return tgt.at[idx].add(src)

def _segment_sum(src, seg, n):
    return jax.ops.segment_sum(src, seg, n)
kernel_name = 'mk_conv_preact_d1_conv_nchw64_r2_933e22'

def setup_inputs(seed: int=0):
    np.random.seed(seed)
    _w = jnp.asarray

    def _rec_inputs():
        import jax
        import jax.numpy as jnp
        _gk = jax.random.key(seed)
        x = -0.0003929 + 0.9999 * jax.random.normal(jax.random.fold_in(_gk, 1), (4, 32, 128, 128), jnp.float32)
        return x
    x = _rec_inputs()

    def _L0_conv_setup():
        import jax, jax.numpy as jnp
        import numpy as np
        DIM = 32
        IMG = 16
        WIN = 16
        HEADS = 8
        PD = 2
        WS = WIN // PD
        L = WS * WS
        E = DIM * PD * PD
        SCALE = (DIM // HEADS) ** (-0.5)
        LN_EPS = 1e-05

        def _rel_pos_index():
            coords = np.stack(np.meshgrid(np.arange(WS), np.arange(WS), indexing='ij'))
            cf = coords.reshape(2, -1)
            rel = (cf[:, :, None] - cf[:, None, :]).transpose(1, 2, 0).copy()
            rel[:, :, 0] += WS - 1
            rel[:, :, 1] += WS - 1
            rel[:, :, 0] *= 2 * WS - 1
            return rel.sum(-1)
        RPI = jnp.asarray(_rel_pos_index().reshape(-1))

        def conv3(x, w, b):
            y = jax.lax.conv_general_dilated(x, w, (1, 1), 'SAME', dimension_numbers=('NCHW', 'OIHW', 'NCHW'))
            return y + b[None, :, None, None]

        def shuffle_invert(x, d):
            B, C, H, W = x.shape
            x = x.reshape(B, C, H // d, d, W // d, d)
            return x.transpose(0, 1, 3, 5, 2, 4).reshape(B, C * d * d, H // d, W // d)

        def pixel_shuffle(x, r):
            B, Cr2, H, W = x.shape
            C = Cr2 // (r * r)
            x = x.reshape(B, C, r, r, H, W)
            return x.transpose(0, 1, 4, 2, 5, 3).reshape(B, C, H * r, W * r)

        def ln(x, g, b):
            m = jnp.mean(x, -1, keepdims=True)
            v = jnp.mean(jnp.square(x - m), -1, keepdims=True)
            return (x - m) * jax.lax.rsqrt(v + LN_EPS) * g + b
        key = jax.random.key(seed)
        ks = jax.random.split(key, 8)
        d = {'x': jax.random.normal(ks[0], (4, DIM, 128, 128), jnp.float32), 'qw': jax.random.normal(ks[1], (DIM, DIM, 3, 3), jnp.float32) * 0.05, 'qb': jnp.zeros((DIM,), jnp.float32), 'kw': jax.random.normal(ks[2], (DIM, DIM, 3, 3), jnp.float32) * 0.05, 'kb': jnp.zeros((DIM,), jnp.float32), 'vw': jax.random.normal(ks[3], (DIM, DIM, 3, 3), jnp.float32) * 0.05, 'vb': jnp.zeros((DIM,), jnp.float32), 'gq': jnp.ones((E,), jnp.float32), 'bq': jnp.zeros((E,), jnp.float32), 'gk': jnp.ones((E,), jnp.float32), 'bk': jnp.zeros((E,), jnp.float32), 'gv': jnp.ones((E,), jnp.float32), 'bv': jnp.zeros((E,), jnp.float32), 'bias_table': jax.random.normal(ks[4], ((2 * WS - 1) ** 2, HEADS), jnp.float32) * 0.02, 'proj_w': jax.random.normal(ks[5], (E, E), jnp.float32) * 0.05, 'proj_b': jnp.zeros((E,), jnp.float32), 'c1w': jax.random.normal(ks[6], (DIM, DIM, 3, 3), jnp.float32) * 0.05, 'c1b': jnp.zeros((DIM,), jnp.float32), 'c2w': jax.random.normal(ks[7], (DIM, DIM, 3, 3), jnp.float32) * 0.05, 'c2b': jnp.zeros((DIM,), jnp.float32)}
        return d
    _L0_conv_all = _L0_conv_setup()
    _L0_conv_in = {k: v for k, v in _L0_conv_all.items() if k in ('qw', 'qb', 'kw', 'kb', 'vw', 'vb', 'gq', 'bq', 'gk', 'bk', 'gv', 'bv', 'bias_table', 'proj_w', 'proj_b', 'c1w', 'c1b', 'c2w', 'c2b')}
    del _L0_conv_all
    return {'x': x, 'L0_conv_qw': _L0_conv_in['qw'], 'L0_conv_qb': _L0_conv_in['qb'], 'L0_conv_kw': _L0_conv_in['kw'], 'L0_conv_kb': _L0_conv_in['kb'], 'L0_conv_vw': _L0_conv_in['vw'], 'L0_conv_vb': _L0_conv_in['vb'], 'L0_conv_gq': _L0_conv_in['gq'], 'L0_conv_bq': _L0_conv_in['bq'], 'L0_conv_gk': _L0_conv_in['gk'], 'L0_conv_bk': _L0_conv_in['bk'], 'L0_conv_gv': _L0_conv_in['gv'], 'L0_conv_bv': _L0_conv_in['bv'], 'L0_conv_bias_table': _L0_conv_in['bias_table'], 'L0_conv_proj_w': _L0_conv_in['proj_w'], 'L0_conv_proj_b': _L0_conv_in['proj_b'], 'L0_conv_c1w': _L0_conv_in['c1w'], 'L0_conv_c1b': _L0_conv_in['c1b'], 'L0_conv_c2w': _L0_conv_in['c2w'], 'L0_conv_c2b': _L0_conv_in['c2b']}

def reference(x, L0_conv_qw, L0_conv_qb, L0_conv_kw, L0_conv_kb, L0_conv_vw, L0_conv_vb, L0_conv_gq, L0_conv_bq, L0_conv_gk, L0_conv_bk, L0_conv_gv, L0_conv_bv, L0_conv_bias_table, L0_conv_proj_w, L0_conv_proj_b, L0_conv_c1w, L0_conv_c1b, L0_conv_c2w, L0_conv_c2b):
    import jax
    import jax.numpy as jnp

    def _L0_conv_ref(x, qw, qb, kw, kb, vw, vb, gq, bq, gk, bk, gv, bv, bias_table, proj_w, proj_b, c1w, c1b, c2w, c2b):
        import jax, jax.numpy as jnp
        import numpy as np
        DIM = 32
        IMG = 16
        WIN = 16
        HEADS = 8
        PD = 2
        WS = WIN // PD
        L = WS * WS
        E = DIM * PD * PD
        SCALE = (DIM // HEADS) ** (-0.5)
        LN_EPS = 1e-05

        def _rel_pos_index():
            coords = np.stack(np.meshgrid(np.arange(WS), np.arange(WS), indexing='ij'))
            cf = coords.reshape(2, -1)
            rel = (cf[:, :, None] - cf[:, None, :]).transpose(1, 2, 0).copy()
            rel[:, :, 0] += WS - 1
            rel[:, :, 1] += WS - 1
            rel[:, :, 0] *= 2 * WS - 1
            return rel.sum(-1)
        RPI = jnp.asarray(_rel_pos_index().reshape(-1))

        def conv3(x, w, b):
            y = jax.lax.conv_general_dilated(x, w, (1, 1), 'SAME', dimension_numbers=('NCHW', 'OIHW', 'NCHW'))
            return y + b[None, :, None, None]

        def shuffle_invert(x, d):
            B, C, H, W = x.shape
            x = x.reshape(B, C, H // d, d, W // d, d)
            return x.transpose(0, 1, 3, 5, 2, 4).reshape(B, C * d * d, H // d, W // d)

        def pixel_shuffle(x, r):
            B, Cr2, H, W = x.shape
            C = Cr2 // (r * r)
            x = x.reshape(B, C, r, r, H, W)
            return x.transpose(0, 1, 4, 2, 5, 3).reshape(B, C, H * r, W * r)

        def ln(x, g, b):
            m = jnp.mean(x, -1, keepdims=True)
            v = jnp.mean(jnp.square(x - m), -1, keepdims=True)
            return (x - m) * jax.lax.rsqrt(v + LN_EPS) * g + b
        B, C, H, W = x.shape
        nH, nW = (H // IMG, W // IMG)
        xw = x.reshape(B, C, nH, IMG, nW, IMG).transpose(0, 2, 4, 1, 3, 5)
        xw = xw.reshape(B * nH * nW, C, IMG, IMG)
        short_cut = xw
        q = shuffle_invert(conv3(xw, qw, qb), PD)
        k = shuffle_invert(conv3(xw, kw, kb), PD)
        v = shuffle_invert(conv3(xw, vw, vb), PD)
        B_ = q.shape[0]
        q = ln(q.reshape(B_, E, L).transpose(0, 2, 1), gq, bq)
        k = ln(k.reshape(B_, E, L).transpose(0, 2, 1), gk, bk)
        v = ln(v.reshape(B_, E, L).transpose(0, 2, 1), gv, bv)
        hd = E // HEADS
        q = q.reshape(B_, L, HEADS, hd).transpose(0, 2, 1, 3) * SCALE
        k = k.reshape(B_, L, HEADS, hd).transpose(0, 2, 1, 3)
        v = v.reshape(B_, L, HEADS, hd).transpose(0, 2, 1, 3)
        attn = jnp.einsum('bhqd,bhkd->bhqk', q, k)
        bias = bias_table[RPI].reshape(L, L, HEADS).transpose(2, 0, 1)
        attn = jax.nn.softmax(attn + bias[None], axis=-1)
        out = jnp.einsum('bhqk,bhkd->bhqd', attn, v)
        out = out.transpose(0, 2, 1, 3).reshape(B_, L, E)
        out = out @ proj_w.T + proj_b
        out = out.transpose(0, 2, 1).reshape(B_, E, WS, WS)
        out = pixel_shuffle(out, PD)
        xw = short_cut + out
        xr = xw.reshape(B, nH, nW, C, IMG, IMG).transpose(0, 3, 1, 4, 2, 5)
        xr = xr.reshape(B, C, H, W)
        y = xr + conv3(jax.nn.gelu(conv3(xr, c1w, c1b), approximate=False), c2w, c2b)
        return y

    def _gn(v, G=32, eps=1e-05):
        B_, C_, H_, W_ = v.shape
        g = v.reshape(B_, G, C_ // G, H_, W_)
        m = jnp.mean(g, axis=(2, 3, 4), keepdims=True)
        s = jnp.var(g, axis=(2, 3, 4), keepdims=True)
        return ((g - m) / jnp.sqrt(s + eps)).reshape(v.shape)

    def _ln_c(v, eps=1e-06):
        m = jnp.mean(v, axis=1, keepdims=True)
        s = jnp.var(v, axis=1, keepdims=True)
        return (v - m) / jnp.sqrt(s + eps)

    def _ln_t(v, eps=1e-05):
        m = jnp.mean(v, axis=-1, keepdims=True)
        s = jnp.var(v, axis=-1, keepdims=True)
        return (v - m) / jnp.sqrt(s + eps)

    def _to_tokens(v):
        B_, C_, H_, W_ = v.shape
        return v.reshape(B_, C_, H_ * W_).transpose(0, 2, 1)

    def _from_tokens(t, like):
        B_, C_, H_, W_ = like.shape
        return t.transpose(0, 2, 1).reshape(B_, C_, H_, W_)
    x = x + _L0_conv_ref(_gn(x), L0_conv_qw, L0_conv_qb, L0_conv_kw, L0_conv_kb, L0_conv_vw, L0_conv_vb, L0_conv_gq, L0_conv_bq, L0_conv_gk, L0_conv_bk, L0_conv_gv, L0_conv_bv, L0_conv_bias_table, L0_conv_proj_w, L0_conv_proj_b, L0_conv_c1w, L0_conv_c1b, L0_conv_c2w, L0_conv_c2b)
    return x

_drawn_inputs = setup_inputs


def setup_inputs(seed=0):
    import zlib

    import numpy as np

    out = dict(_drawn_inputs(seed))
    spreads = {'L0_conv_qb': (0.0, 0.407),
     'L0_conv_kb': (0.0, 0.8),
     'L0_conv_vb': (0.0, 0.1),
     'L0_conv_gq': (1.0, 0.2),
     'L0_conv_bq': (0.0, 0.503),
     'L0_conv_gk': (1.0, 0.2),
     'L0_conv_bk': (0.0, 2.0),
     'L0_conv_gv': (1.0, 0.6),
     'L0_conv_bv': (0.0, 0.1),
     'L0_conv_proj_b': (0.0, 0.1),
     'L0_conv_c1b': (0.0, 0.332),
     'L0_conv_c2b': (0.0, 0.1)}
    factors = {'L0_conv_bias_table': 29.666}
    for name, (base, spread) in spreads.items():
        noise = np.random.default_rng([zlib.crc32(name.encode()), seed]).standard_normal(out[name].shape)
        drawn = base * np.exp(spread * noise) if base else spread * noise
        out[name] = jnp.asarray(drawn.astype(out[name].dtype))
    for name, factor in factors.items():
        out[name] = (out[name] * factor).astype(out[name].dtype)
    return out
```

```python
from contextlib import ExitStack

import numpy as np

import concourse.bass as bass
from concourse import mybir

F32 = mybir.dt.float32
F16 = mybir.dt.float16
BF16 = mybir.dt.bfloat16
ALU = mybir.AluOpType
ACT = mybir.ActivationFunctionType
AX = mybir.AxisListType
RMAX = bass.bass_isa.ReduceOp.max

P = 128
B, C, IMG = 4, 32, 128
WIN = 16
TS = WIN // 2
TOK = TS * TS
E = 4 * C
HEADS = 8
HD = E // HEADS
HP = HEADS // 2
NROW = IMG // WIN
NWIN = IMG // WIN
PAIRS = NROW * NWIN // 2
G = IMG // 2
NT = G * G
HALO = TS + 1
QKV = 3 * E
VW = 2 * HD + 1
GN_EPS = 1e-5
LN_EPS = 1e-5
SCALE = (C // HEADS) ** -0.5
XN_UP = 64.0
W_TOP = 16.0
QK_TOP = 8192.0
LN_BOUND = float(E) ** 0.5

GQ, BQ, GK, BK, EVEN, ODD, GV, BV, PB, C1B, C2B = range(11)
NVEC = 11

T1R = 5
T1N = (G + 1) // T1R
T2R = 8
T2N = G // T2R


def conv_attention(nc, x_al, x_sh, mask, wqkv, bqkv, bias_t, proj_t, vecs, w1, w2, ident, sel_mean, sel_ones, tok_ident, out):
    with ExitStack() as ctx:
        def sb(name, shape, dt=F32):
            return ctx.enter_context(nc.sbuf_tensor(name, shape, dt))

        def psum(name, shape, dt=F32):
            return ctx.enter_context(nc.psum_tensor(name, shape, dt))

        def sem(name):
            return ctx.enter_context(nc.semaphore(name))

        y_ps = [psum(f"y_ps{i}", [P, 512]) for i in range(2)]
        t_ps = psum("t_ps", [P, 2, 2, P])
        s_ps = psum("s_ps", [P, 2, 512])
        pt_ps = psum("pt_ps", [P, HP, P])
        o_ps = psum("o_ps", [P, HP, 2, VW])
        ox_ps = psum("ox_ps", [P, 512])

        vec = sb("vec", [P, NVEC])
        idf = sb("idf", [P, P])
        selm = sb("selm", [P, P])
        tokid = sb("tokid", [P, TOK])
        maskt = sb("maskt", [P, HALO * HALO])
        ones_f = sb("ones_f", [P, P])
        ones_b = sb("ones_b", [P, P], BF16)
        wst = sb("wst", [P, 4, QKV])
        w_hi = sb("w_hi", [P, 4, QKV], F16)
        w_lo = sb("w_lo", [P, 4, QKV], F16)
        bst = sb("bst", [P, QKV])
        b_parts = sb("b_parts", [P, QKV], BF16)
        b_tmp = sb("b_tmp", [P, QKV], BF16)
        biasS = sb("biasS", [P, 2, HP * TOK])
        projw = sb("projw", [P, P])
        projg = sb("projg", [P, P])
        w1s = sb("w1s", [P, 4, P])
        w2s = sb("w2s", [P, 4, P])
        amax = sb("amax", [P, 8])
        amax_all = sb("amax_all", [P, 8])
        cw = sb("cw", [P, 3])
        sw = sb("sw", [P, 3])
        eps_y = sb("eps_y", [P, 3])
        cqk = sb("cqk", [P, 4])
        qk_aff = sb("qk_aff", [P, 4])
        s_inv = sb("s_inv", [P, 1])
        neg_half = sb("neg_half", [P, 4])
        pbias = sb("pbias", [P, 1])
        wait_slot = sb("wait_slot", [P, 1])

        xst = sb("xst", [P, NT])
        gst = sb("gst", [P, 8, 6])
        gmv = sb("gmv", [P, 2])
        gm = sb("gm", [P, 8])
        maskr = sb("maskr", [P, HALO * HALO])
        xr = sb("xr", [P, G + 2, G + 2])
        hgrid = sb("hgrid", [P, G + 1, G + 1])
        xf = [sb(f"xf{i}", [P, 512]) for i in range(2)]
        yt = [sb(f"yt{i}", [P, 512]) for i in range(2)]

        xs = [sb(f"xs{i}", [P, NWIN, HALO * HALO]) for i in range(2)]
        xnf = [sb(f"xnf{i}", [P, NWIN, HALO * HALO]) for i in range(2)]
        x_hi = [sb(f"x_hi{i}", [P, 4, NWIN * TOK], F16) for i in range(2)]
        x_lo = [sb(f"x_lo{i}", [P, 4, NWIN * TOK], F16) for i in range(2)]
        ot = [sb(f"ot{i}", [P, 512]) for i in range(2)]

        ln_st = [sb(f"ln_st{i}", [P, 3, 6]) for i in range(2)]
        ln_mv = [sb(f"ln_mv{i}", [P, 3, 2]) for i in range(2)]
        ln_ve = [sb(f"ln_ve{i}", [P, 3]) for i in range(2)]
        ln_rs = [sb(f"ln_rs{i}", [P, 3]) for i in range(2)]
        ln_nm = [sb(f"ln_nm{i}", [P, 3]) for i in range(2)]
        ln_nr = [sb(f"ln_nr{i}", [P, 3]) for i in range(2)]
        qk_n = [sb(f"qk_n{i}", [P, 2, P]) for i in range(2)]
        v_bd = [sb(f"v_bd{i}", [P, HP, 2, VW]) for i in range(8)]
        sc = [sb(f"sc{i}", [P, HP, 2, TOK]) for i in range(4)]
        mx = [sb(f"mx{i}", [P, HP, 2]) for i in range(2)]
        pt = [sb(f"pt{i}", [P, HP, P]) for i in range(2)]
        rs = [sb(f"rs{i}", [P, HP, 2]) for i in range(2)]
        on = [sb(f"on{i}", [P, 2, 2, HP, HD]) for i in range(2)]
        qk_t = [sb(f"qk_t{i}", [P, 2, 2 * P]) for i in range(2)]
        q_hi = [sb(f"q_hi{i}", [P, 4, 2, TOK], F16) for i in range(2)]
        q_lo = [sb(f"q_lo{i}", [P, 4, 2, TOK], F16) for i in range(2)]
        k_hi = [sb(f"k_hi{i}", [P, 2 * P], F16) for i in range(2)]
        k_lo = [sb(f"k_lo{i}", [P, 2 * P], F16) for i in range(2)]

        loaded_consts = sem("loaded_consts")
        setup_dve = sem("setup_dve")
        setup_pool = sem("setup_pool")
        setup_act = sem("setup_act")
        setup_pe = sem("setup_pe")
        weights_ready = sem("weights_ready")
        loaded_xst = sem("loaded_xst")
        loaded_xs = [sem(f"loaded_xs{i}") for i in range(2)]
        gn_chain = sem("gn_chain")
        gn_pe = sem("gn_pe")
        gn_dve = sem("gn_dve")
        gn_pool = sem("gn_pool")
        image_scaled = sem("image_scaled")
        xr_begun = sem("xr_begun")
        xn_done = sem("xn_done")
        xhi_done = sem("xhi_done")
        xlo_done = sem("xlo_done")
        conv_done = sem("conv_done")
        ln_stats = sem("ln_stats")
        ln_moments = sem("ln_moments")
        ln_var_eps = sem("ln_var_eps")
        ln_scales = sem("ln_scales")
        ln_qk = sem("ln_qk")
        ln_v = sem("ln_v")
        tr_done = sem("tr_done")
        qkt_done = sem("qkt_done")
        qk_hi_done = sem("qk_hi_done")
        qk_split = sem("qk_split")
        scores_done = sem("scores_done")
        biased = sem("biased")
        maxed = sem("maxed")
        shifted = sem("shifted")
        exped = sem("exped")
        ptr_done = sem("ptr_done")
        pt_copied = sem("pt_copied")
        pv_done = sem("pv_done")
        sums_inv = sem("sums_inv")
        normed = sem("normed")
        ot_done = sem("ot_done")
        ot_copied = sem("ot_copied")
        proj_done = sem("proj_done")
        xr_added = sem("xr_added")
        c1_done = sem("c1_done")
        gelu_done = sem("gelu_done")
        h_border = sem("h_border")
        c2_done = sem("c2_done")
        xf_loaded = [sem(f"xf_loaded{i}") for i in range(2)]
        res_added = sem("res_added")
        ln_pow = sem("ln_pow")
        h_rows = sem("h_rows")
        scores_bank = sem("scores_bank")
        y_ready = sem("y_ready")
        stored = [sem(f"stored{i}") for i in range(2)]
        NCONST = 13
        BODY, BODIES = 8, 2
        PROLOGUE = range(-4, BODY)
        EPILOGUE = range(BODY * (1 + BODIES), PAIRS + 4)
        head_pair = [hp for bank in range(2) for hp in range(bank, HP, 2)]
        c_ps = [y_ps[0][:, :], y_ps[1][:, :], s_ps[:, 0, :], s_ps[:, 1, :]]

        def steps(e, b, step):
            for i in PROLOGUE:
                step(i, b * PAIRS, b * (PAIRS // 2), b * NROW, b * (NROW // 2), 0)
            with e.Fori(0, BODIES) as t:
                for i in range(BODY, 2 * BODY):
                    step(i, b * PAIRS + t * BODY, b * (PAIRS // 2) + t * (BODY // 2), b * NROW + t * (BODY // 4),
                         b * (NROW // 2) + t * (BODY // 8), t * (BODY // 4))
            for i in EPILOGUE:
                step(i, b * PAIRS, b * (PAIRS // 2), b * NROW, b * (NROW // 2), 0)

        def at_offset(t, a):
            return t[:, a, :].rearrange("p (w i j) -> p w i j", w=NWIN, i=TS)

        def shifted_groups(t, a):
            g = t[:, :, :].rearrange("p w (i j) -> p w i j", i=HALO)
            return g[:, :, a // 2:a // 2 + TS, a % 2:a % 2 + TS]

        parts_of = ((0,), (1,), (2, 3), ())

        def has(n):
            return 0 <= n < PAIRS

        block = ctx.enter_context(nc.Block())

        @block.sync
        def _(sp):
            for dst, src in ((vec, vecs), (idf, ident), (selm, sel_mean), (ones_f, sel_ones), (tokid, tok_ident),
                             (maskt, mask), (wst, wqkv), (bst, bqkv), (biasS, bias_t), (projw, proj_t),
                             (w1s, w1), (w2s, w2)):
                full = tuple(slice(None) for _ in dst.shape)
                sp.dma_start(dst[full], src).then_inc(loaded_consts, 16)
            with sp.Fori(0, B) as b:
                sp.wait_ge(xr_begun, b + 1)
                sp.dma_start(xst[:, :], x_al[b]).then_inc(loaded_xst, 16)
                for r in range(NROW):
                    if r >= 2:
                        sp.wait_ge(xn_done, b * NROW + r)
                    else:
                        sp.wait_ge(xn_done, b * NROW + 1)
                    sp.dma_start(xs[r % 2][:, :, :], x_sh[b, :, r, :].rearrange("p (w t) -> p w t", w=NWIN)).then_inc(
                        loaded_xs[r % 2], 16)
                for t in range(T2N):
                    if t >= 2:
                        sp.wait_ge(y_ready, b * T2N + (t - 1) + 1)
                    else:
                        sp.wait_ge(y_ready, b * T2N + 1)
                    sp.dma_start(xf[t % 2][:, :], x_al[b, :, 512 * t:512 * (t + 1)]).then_inc(xf_loaded[t % 2], 16)
                    if t >= 1:
                        sp.wait_ge(y_ready, b * T2N + t + 1)
                        sp.dma_start(out[b, :, 512 * (t - 1):512 * t], yt[(t - 1) % 2][:, :]).then_inc(
                            stored[(t - 1) % 2], 16)
                sp.wait_ge(y_ready, b * T2N + T2N + 1)
                sp.dma_start(out[b, :, 512 * (T2N - 1):], yt[(T2N - 1) % 2][:, :]).then_inc(stored[(T2N - 1) % 2], 16)
            for i in range(2):
                sp.wait_ge(stored[i], 16 * B * T2N // 2 + 16)

        @block.vector
        def _(v):
            n = [0]

            def link(ins):
                n[0] += 1
                ins.then_inc(setup_dve, 1)
                v.wait_ge(setup_dve, n[0])

            v.memset(neg_half[:, :], -0.5).then_inc(xr_begun, 1)
            v.memset(wait_slot[:, :], 0.0).then_inc(xn_done, 1)
            v.memset(s_inv[:, :], 0.0).then_inc(res_added, 1)
            v.memset(pbias[:, :], 0.0).then_inc(y_ready, 1)
            v.memset(maskr[:, :], 0.0).then_inc(stored[0], 16)
            v.memset(gm[:, :], 0.0).then_inc(stored[1], 16)
            v.memset(xr[:, :, :], 0.0)
            for t in v_bd:
                v.memset(t[:, :, :, :], 0.0)
            for t in on:
                v.memset(t[:, :, :, :, :], 0.0)
            link(v.memset(hgrid[:, :, :], 0.0))
            for t in v_bd:
                v.memset(t[0:64, :, 0, VW - 1:VW], 1.0)
                v.memset(t[64:128, :, 1, VW - 1:VW], 1.0)
            v.wait_ge(loaded_consts, 16 * 12)
            for t in range(3):
                v.tensor_reduce(amax[:, t:t + 1], wst[:, :, E * t:E * (t + 1)], AX.XY, ALU.max,
                                apply_absolute_value=True)
            for j in range(4):
                ins = v.tensor_reduce(amax[:, 3 + j:4 + j], vec[:, j:j + 1], AX.X, ALU.max, apply_absolute_value=True)
            link(ins)
            v.tensor_copy(ones_b[:, :], ones_f[:, :]).then_inc(weights_ready, 1)
            v.wait_ge(setup_pool, 1)
            link(v.tensor_scalar(sw[:, :], amax_all[:, 0:3], 1e-15, None, ALU.max))
            link(v.reciprocal(cw[:, :], sw[:, :]))
            link(v.tensor_scalar(sw[:, :], cw[:, :], W_TOP, None, ALU.mult))
            link(v.tensor_scalar(cw[:, :], sw[:, :], XN_UP, None, ALU.mult))
            link(v.tensor_tensor(eps_y[:, :], cw[:, :], cw[:, :], ALU.mult))
            link(v.tensor_scalar(eps_y[:, :], eps_y[:, :], LN_EPS, None, ALU.mult))
            for j in range(2):
                g0 = 3 + 2 * j
                link(v.tensor_scalar(cqk[:, j:j + 1], amax_all[:, g0:g0 + 1], LN_BOUND, 1e-15, ALU.mult, ALU.max))
                link(v.tensor_tensor(cqk[:, 2 + j:3 + j], cqk[:, j:j + 1], amax_all[:, g0 + 1:g0 + 2], ALU.add))
            link(v.reciprocal(cqk[:, 0:2], cqk[:, 2:4]))
            link(v.tensor_scalar(cqk[:, 0:2], cqk[:, 0:2], QK_TOP, None, ALU.mult))
            for j in range(2):
                link(v.tensor_scalar(qk_aff[:, 2 * j:2 * j + 2], vec[:, 2 * j:2 * j + 2], cqk[:, j:j + 1], None,
                                     ALU.mult))
            link(v.tensor_tensor(s_inv[:, :], cqk[:, 2:3], cqk[:, 3:4], ALU.mult))
            link(v.tensor_scalar(s_inv[:, :], s_inv[:, :], SCALE / (QK_TOP * QK_TOP), None, ALU.mult))
            for t in range(3):
                cols = slice(E * t, E * (t + 1))
                link(v.tensor_scalar(wst[:, :, cols], wst[:, :, cols], sw[:, t:t + 1], None, ALU.mult))
                link(v.tensor_scalar(bst[:, cols], bst[:, cols], cw[:, t:t + 1], None, ALU.mult))
            link(v.tensor_copy(w_hi[:, :, :], wst[:, :, :]))
            link(v.tensor_tensor(w_lo[:, :, :], wst[:, :, :], w_hi[:, :, :], ALU.subtract))
            for j in range(3):
                link(v.tensor_copy(b_tmp[:, :], bst[:, :]))
                link(v.tensor_copy(b_parts[32 * j:32 * j + 32, :], b_tmp[32 * j:32 * j + 32, :]))
                link(v.tensor_tensor(bst[:, :], bst[:, :], b_tmp[:, :], ALU.subtract))
            link(v.tensor_scalar(projg[:, :], projw[:, :], vec[:, GV:GV + 1], None, ALU.mult))
            v.wait_ge(setup_pe, 1)
            link(v.tensor_tensor(pbias[:, :], ox_ps[:, 0:1], vec[:, PB:PB + 1], ALU.add))
            v.tensor_copy(amax[:, 0:1], amax_all[:, 0:1]).then_inc(weights_ready, 1)

            with v.Fori(0, B) as b:
                v.wait_ge(loaded_xst, 16 * b + 16)
                for j in range(8):
                    ins = v.bn_stats(gst[:, j, :], xst[:, 512 * j:512 * (j + 1)])
                ins.then_inc(gn_chain, 1)
                v.wait_ge(gn_chain, b * 7 + 1)
                v.tensor_copy(wait_slot[:, :], vec[:, 0:1])
                v.bn_aggr(gmv[:, :], gst[:, :, :]).then_inc(gn_dve, 1)
                v.wait_ge(gn_pe, b * 2 + 1)
                v.tensor_copy(gm[:, 0:1], ox_ps[:, 0:1]).then_inc(gn_chain, 1)
                v.wait_ge(gn_chain, b * 7 + 2)
                v.tensor_tensor(gm[:, 1:2], gmv[:, 0:1], gm[:, 0:1], ALU.subtract).then_inc(gn_chain, 1)
                v.wait_ge(gn_chain, b * 7 + 3)
                v.scalar_tensor_tensor(gm[:, 2:3], gm[:, 1:2], gm[:, 1:2], gmv[:, 1:2], ALU.mult, ALU.add).then_inc(
                    gn_dve, 1)
                v.wait_ge(gn_pe, b * 2 + 2)
                v.tensor_scalar(gm[:, 3:4], ox_ps[:, 0:1], GN_EPS, None, ALU.add).then_inc(gn_dve, 1)
                v.wait_ge(gn_pool, b + 1)
                v.tensor_scalar(maskr[:, :], maskt[:, :], gm[:, 4:5], XN_UP, ALU.mult, ALU.mult).then_inc(gn_chain, 1)
                v.tensor_tensor(gm[:, 5:6], gm[:, 0:1], gm[:, 4:5], ALU.mult).then_inc(gn_chain, 1)
                v.wait_ge(gn_chain, b * 7 + 5)
                v.tensor_tensor(gm[:, 6:7], pbias[:, :], gm[:, 5:6], ALU.subtract).then_inc(gn_chain, 1)
                v.wait_ge(gn_chain, b * 7 + 6)
                v.tensor_scalar(xr[:, 1:G + 1, 1:G + 1], xst[:, :].rearrange("p (i j) -> p i j", i=G),
                                gm[:, 4:5], gm[:, 6:7], ALU.mult, ALU.add).then_inc(xr_begun, 1)
                v.tensor_copy(gm[:, 7:8], gm[:, 6:7]).then_inc(gn_chain, 1)

                def row(r, r0, rr0):
                    v.wait_ge(loaded_xs[r % 2], (rr0 + (r // 2 + 1)) * 16)
                    if r >= 2:
                        v.wait_ge(xlo_done, (r0 + (r - 1)) * 4)
                    v.scalar_tensor_tensor(
                        xnf[r % 2][:, :, :], xs[r % 2][:, :, :], gm[:, 0:1],
                        maskr[:, :].unsqueeze(1).to_broadcast([P, NWIN, HALO * HALO]),
                        ALU.subtract, ALU.mult).then_inc(xn_done, 1)

                def step(i, p0, h0, r0, rr0, row0):
                    if i % 4 == 0 and 2 <= (i + 8) // 4 < NROW:
                        row((i + 8) // 4, r0, rr0)
                    if i % 2 == 1 and has(i + 1):
                        h = (i + 1) // 2
                        v.wait_ge(qkt_done, h0 + (h + 1))
                        if h >= 2:
                            v.wait_ge(scores_done, p0 + (2 * h - 2))
                        for par in range(2):
                            v.tensor_scalar(q_hi[h % 2][:, :, par, :],
                                            qk_t[h % 2][:, 0, :].rearrange("p (w t) -> p w t", w=4), vec[:, EVEN + par:EVEN + par + 1], None, ALU.mult)
                        v.tensor_copy(k_hi[h % 2][:, :], qk_t[h % 2][:, 1, :]).then_inc(qk_hi_done, 1)
                        v.wait_ge(qk_hi_done, h0 + (h + 1))
                        for par in range(2):
                            v.scalar_tensor_tensor(q_lo[h % 2][:, :, par, :],
                                                   qk_t[h % 2][:, 0, :].rearrange("p (w t) -> p w t", w=4),
                                                   vec[:, EVEN + par:EVEN + par + 1], q_hi[h % 2][:, :, par, :],
                                                   ALU.mult, ALU.subtract)
                        v.tensor_tensor(k_lo[h % 2][:, :], qk_t[h % 2][:, 1, :], k_hi[h % 2][:, :],
                                        ALU.subtract).then_inc(qk_split, 1)
                    if has(i + 4):
                        m = i + 4
                        v.wait_ge(conv_done, p0 + (m + 1))
                        if m >= 2:
                            v.wait_ge(ln_scales, p0 + (m - 1))
                        for t in range(3):
                            ins = v.bn_stats(ln_st[m % 2][:, t, :], y_ps[m % 2][:, E * t:E * (t + 1)])
                        ins.then_inc(ln_stats, 1)
                        v.wait_ge(ln_stats, p0 + (m + 1))
                        v.tensor_copy(wait_slot[:, :], vec[:, 0:1])
                        for t in range(3):
                            ins = v.bn_aggr(ln_mv[m % 2][:, t, :], ln_st[m % 2][:, t, :])
                        ins.then_inc(ln_moments, 1)
                    if i % 4 == 3 and i >= 7:
                        r = (i - 7) // 4
                        v.wait_ge(proj_done, r0 + (r + 1))
                        rows = xr[:, bass.ds((row0 + r) * TS + 1, TS), 1:G + 1].rearrange("p i (w j) -> p w i j", w=NWIN)
                        v.tensor_tensor(rows, rows, ox_ps[:, :].rearrange("p (w i j) -> p w i j", w=NWIN, i=TS),
                                        ALU.add).then_inc(xr_added, 1)
                    if has(i):
                        v.wait_ge(scores_done, p0 + (i + 1))
                        if i >= 4:
                            v.wait_ge(ptr_done, p0 + (i - 3))
                        v.scalar_tensor_tensor(sc[i % 4][:, :, :, :].rearrange("p (a h) w k -> p a (h w k)", a=2),
                                               s_ps[:, :, 0:256], s_inv[:, 0:1], biasS[:, :, :],
                                               ALU.mult, ALU.add).then_inc(biased, 1)
                        v.wait_ge(biased, p0 + (i + 1))
                        if i >= 2:
                            v.wait_ge(shifted, p0 + (i - 1))
                        v.tensor_reduce(mx[i % 2][:, :, :], sc[i % 4][:, :, :, :], AX.X, ALU.max).then_inc(maxed, 1)
                    if has(i - 2):
                        m = i - 2
                        v.wait_ge(pv_done, p0 + (m + 1))
                        v.reciprocal(rs[m % 2][:, :, :], o_ps[:, :, :, VW - 1]).then_inc(sums_inv, 1)
                        v.wait_ge(sums_inv, p0 + (m + 1))
                        if m >= 2:
                            v.wait_ge(ot_done, p0 + (m - 1))
                        for par in range(2):
                            q = slice(64 * par, 64 * par + 64)
                            ins = v.tensor_tensor(
                                on[m % 2][q, :, par, :, :],
                                o_ps[q, :, :, HD * par:HD * (par + 1)].rearrange("p h w d -> p w h d"),
                                rs[m % 2][q, :, :].rearrange("p h w -> p w h").unsqueeze(3).to_broadcast(
                                    [64, 2, HP, HD]),
                                ALU.mult)
                        ins.then_inc(normed, 1)

                row(0, b * NROW, b * (NROW // 2))
                row(1, b * NROW, b * (NROW // 2))
                steps(v, b, step)
                v.wait_ge(gelu_done, b * T1N + T1N)
                v.memset(hgrid[64:128, 0:1, :], 0.0)
                v.memset(hgrid[0:64, G:G + 1, :], 0.0).then_inc(h_rows, 1)
                v.wait_ge(h_rows, b + 1)
                for q in range(4):
                    out_of = 0 if q % 2 else G
                    ins = v.memset(hgrid[32 * q:32 * q + 32, :, out_of:out_of + 1], 0.0)
                ins.then_inc(h_border, 1)
                for t in range(T2N):
                    v.wait_ge(c2_done, b * T2N + (t + 1))
                    v.wait_ge(stored[t % 2], (b * (T2N // 2) + t // 2 + 1) * 16)
                    v.scalar_tensor_tensor(yt[t % 2][:, :].rearrange("p (i j) -> p i j", i=T2R),
                                           c_ps[t % 4].rearrange("p (i j) -> p i j", i=T2R), vec[:, C2B:C2B + 1],
                                           xr[:, 1 + T2R * t:1 + T2R * (t + 1), 1:G + 1],
                                           ALU.add, ALU.add).then_inc(res_added, 1)
                    v.wait_ge(res_added, b * T2N + (t + 1) + 1)
                    v.wait_ge(xf_loaded[t % 2], (b * (T2N // 2) + (t // 2 + 1)) * 16)
                    v.tensor_tensor(yt[t % 2][:, :], yt[t % 2][:, :], xf[t % 2][:, :], ALU.add).then_inc(y_ready, 1)

        @block.gpsimd
        def _(pool):
            pool.wait_ge(setup_dve, 2)
            pool.partition_all_reduce(amax_all[:, 0:7], amax[:, 0:7], P, RMAX).then_inc(setup_pool, 1)
            pool.wait_ge(weights_ready, 2)
            with pool.Fori(0, B) as b:
                pool.wait_ge(gn_dve, b * 3 + 3)
                pool.tensor_tensor(gm[:, 4:5], gm[:, 3:4], neg_half[:, 0:1], ALU.pow).then_inc(gn_pool, 1)

                def part(r, a, p0, r0):
                    pool.wait_ge(xhi_done, (r0 + r) * 4 + a + 1)
                    if r >= 2:
                        pool.wait_ge(conv_done, p0 + (4 * r - 4))
                    pool.tensor_tensor(at_offset(x_lo[r % 2], a), shifted_groups(xnf[r % 2], a),
                                       at_offset(x_hi[r % 2], a), ALU.subtract).then_inc(xlo_done, 1)

                def step(i, p0, h0, r0, rr0, row0):
                    if has(i + 4):
                        m = i + 4
                        j = m % 2
                        pool.wait_ge(ln_moments, p0 + (m + 1))
                        if m >= 2:
                            pool.wait_ge(ln_v, p0 + (m - 1))
                        pool.tensor_tensor(ln_ve[j][:, :], ln_mv[j][:, :, 1], eps_y[:, :], ALU.add)
                        pool.tensor_scalar(ln_nm[j][:, :], ln_mv[j][:, :, 0], -1.0, None, ALU.mult).then_inc(
                            ln_var_eps, 1)
                        pool.wait_ge(ln_var_eps, p0 + (m + 1))
                        pool.tensor_tensor(ln_rs[j][:, :], ln_ve[j][:, :], neg_half[:, 0:3], ALU.pow).then_inc(
                            ln_pow, 1)
                        pool.wait_ge(ln_pow, p0 + (m + 1))
                        pool.tensor_tensor(ln_nr[j][:, :], ln_nm[j][:, :], ln_rs[j][:, :], ALU.mult).then_inc(
                            ln_scales, 1)
                    if has(i):
                        pool.wait_ge(maxed, p0 + (i + 1))
                        pool.tensor_tensor(sc[i % 4][:, :, :, :], sc[i % 4][:, :, :, :],
                                           mx[i % 2][:, :, :].unsqueeze(3).to_broadcast([P, HP, 2, TOK]),
                                           ALU.subtract).then_inc(shifted, 1)
                    if 2 <= (i + 8) // 4 < NROW:
                        for a in parts_of[i % 4]:
                            part((i + 8) // 4, a, p0, r0)

                for r in range(2):
                    for a in range(4):
                        part(r, a, b * PAIRS, b * NROW)
                steps(pool, b, step)

        @block.scalar
        def _(act):
            act.wait_ge(weights_ready, 2)
            with act.Fori(0, B) as b:
                def part(r, a, p0, r0):
                    act.wait_ge(xn_done, r0 + (r + 1) + 1)
                    if r >= 2:
                        act.wait_ge(conv_done, p0 + (4 * r - 4))
                    act.activation(at_offset(x_hi[r % 2], a), shifted_groups(xnf[r % 2], a), ACT.Copy).then_inc(
                        xhi_done, 1)

                def step(i, p0, h0, r0, rr0, row0):
                    if 2 <= (i + 8) // 4 < NROW:
                        for a in parts_of[i % 4]:
                            part((i + 8) // 4, a, p0, r0)
                    if i % 2 == 0 and has(i + 2):
                        h = (i + 2) // 2
                        act.wait_ge(tr_done, p0 + (2 * h + 2))
                        if h >= 2:
                            act.wait_ge(qk_split, h0 + (h - 1))
                        for t in range(2):
                            ins = act.activation(qk_t[h % 2][:, t, :], t_ps[:, t, :, :].rearrange("p a n -> p (a n)"),
                                                 ACT.Identity, scale=qk_aff[:, 2 * t:2 * t + 1],
                                                 bias=qk_aff[:, 2 * t + 1:2 * t + 2])
                        ins.then_inc(qkt_done, 1)
                    if has(i - 1):
                        m = i - 1
                        act.wait_ge(ptr_done, p0 + (m + 1))
                        if m >= 2:
                            act.wait_ge(pv_done, p0 + (m - 1))
                        act.activation(pt[m % 2][:, :, :], pt_ps[:, :, :], ACT.Copy).then_inc(pt_copied, 1)
                    if i % 4 == 2 and i >= 6:
                        r = (i - 6) // 4
                        act.wait_ge(ot_done, p0 + (4 * r + 4))
                        if r >= 2:
                            act.wait_ge(proj_done, r0 + (r - 1))
                        act.activation(ot[r % 2][:, :], ox_ps[:, :], ACT.Copy).then_inc(ot_copied, 1)
                    if has(i + 4):
                        m = i + 4
                        j = m % 2
                        act.wait_ge(ln_scales, p0 + (m + 1))
                        if m >= 2:
                            act.wait_ge(tr_done, p0 + (m - 1))
                        for t in range(2):
                            ins = act.activation(qk_n[j][:, t, :], y_ps[j][:, E * t:E * (t + 1)], ACT.Identity,
                                                 scale=ln_rs[j][:, t:t + 1], bias=ln_nr[j][:, t:t + 1])
                        ins.then_inc(ln_qk, 1)
                        if m >= 8:
                            act.wait_ge(pv_done, p0 + (m - 7))
                        for w in range(2):
                            q = slice(64 * w, 64 * w + 64)
                            ins = act.activation(
                                v_bd[m % 8][q, :, w, 0:2 * HD],
                                y_ps[j][q, 2 * E:3 * E].rearrange("p (h d) -> p h d", h=HP), ACT.Identity,
                                scale=ln_rs[j][q, 2:3], bias=ln_nr[j][q, 2:3])
                        ins.then_inc(ln_v, 1)
                    if has(i):
                        act.wait_ge(shifted, p0 + (i + 1))
                        act.activation(sc[i % 4][:, :, :, :], sc[i % 4][:, :, :, :], ACT.Exp).then_inc(exped, 1)
                for r in range(2):
                    for a in range(4):
                        part(r, a, b * PAIRS, b * NROW)
                steps(act, b, step)
                for t in range(T1N):
                    act.wait_ge(c1_done, b * T1N + (t + 1))
                    act.activation(hgrid[:, T1R * t:T1R * (t + 1), :],
                                   c_ps[t % 4][:, 0:T1R * (G + 1)].rearrange("p (i j) -> p i j", i=T1R), ACT.Gelu,
                                   bias=vec[:, C1B:C1B + 1]).then_inc(gelu_done, 1)

        @block.tensor
        def _(pe):
            pe.wait_ge(loaded_consts, 16 * 12)
            pe.matmul(ox_ps[:, 0:1], projw[:, :], vec[:, BV:BV + 1], start=True, stop=True).then_inc(setup_pe, 1)
            pe.wait_ge(weights_ready, 2)
            with pe.Fori(0, B) as b:
                pe.wait_ge(gn_dve, b * 3 + 1)
                pe.matmul(ox_ps[:, 0:1], selm[:, :], gmv[:, 0:1], start=True, stop=True).then_inc(gn_pe, 1)
                pe.wait_ge(gn_dve, b * 3 + 2)
                pe.matmul(ox_ps[:, 0:1], selm[:, :], gm[:, 2:3], start=True, stop=True).then_inc(gn_pe, 1)

                def step(i, p0, h0, r0, rr0, row0):
                    if i % 4 == 3 and i >= 7:
                        r = (i - 7) // 4
                        pe.wait_ge(ot_copied, r0 + (r + 1))
                        pe.matmul(ox_ps[:, :], projg[:, :], ot[r % 2][:, :], start=True, stop=True).then_inc(
                            proj_done, 1)
                    if has(i + 4):
                        m = i + 4
                        r, s = m // 4, m % 4
                        if s == 0:
                            pe.wait_ge(xlo_done, (r0 + (r + 1)) * 4)
                        if m >= 2:
                            pe.wait_ge(ln_v, p0 + (m - 1))
                        else:
                            pe.wait_ge(res_added, b * T2N + 1)
                        y = y_ps[m % 2][:, 0:QKV]
                        pe.matmul(y, ones_b[0:96, :], b_parts[0:96, :], start=True, stop=False)
                        for a in range(4):
                            for xx, ww in ((x_hi, w_hi), (x_hi, w_lo), (x_lo, w_hi)):
                                ins = pe.matmul(y, xx[r % 2][:, a, P * s:P * (s + 1)], ww[:, a, :],
                                                start=False, stop=(a == 3 and xx is x_lo))
                        ins.then_inc(conv_done, 1)
                    if has(i + 3):
                        m = i + 3
                        pe.wait_ge(ln_qk, p0 + (m + 1))
                        if m % 2 == 0 and m >= 2:
                            pe.wait_ge(qkt_done, h0 + m // 2)
                        for t in range(2):
                            ins = pe.transpose(t_ps[:, t, m % 2, :], qk_n[m % 2][:, t, :], idf[:, :])
                        ins.then_inc(tr_done, 1)
                    if has(i):
                        h = i // 2
                        pe.wait_ge(qk_split, h0 + (h + 1))
                        if i >= 1:
                            pe.wait_ge(biased, p0 + i)
                        for hp in range(HP):
                            rows = slice(32 * hp, 32 * hp + 32)
                            if hp >= 2:
                                pe.wait_ge(scores_bank, (p0 + i) * 2 + (hp - 1))
                            for w in range(2):
                                tok = slice(P * (i % 2) + TOK * w, P * (i % 2) + TOK * (w + 1))
                                c0 = (hp // 2) * 128 + TOK * w
                                for n, (qq, kk) in enumerate(((q_hi, k_hi), (q_hi, k_lo), (q_lo, k_hi))):
                                    ins = pe.matmul(s_ps[:, hp % 2, c0:c0 + TOK], qq[h % 2][rows, 2 * (i % 2) + w, :, :].rearrange("p a t -> p (a t)"),
                                                    kk[h % 2][rows, tok], start=(n == 0), stop=(n == 2))
                            if hp < 2:
                                ins.then_inc(scores_bank, 1)
                        ins.then_inc(scores_done, 1)
                    if has(i - 1):
                        m = i - 1
                        pe.wait_ge(exped, p0 + (m + 1))
                        if m >= 1:
                            pe.wait_ge(pt_copied, p0 + m)
                        for g in range(HP):
                            ins = pe.transpose(pt_ps[:, g, :], sc[m % 4][:, g, :, :].rearrange("p w k -> p (w k)"),
                                               idf[:, :])
                        ins.then_inc(ptr_done, 1)
                    if has(i - 2):
                        m = i - 2
                        pe.wait_ge(pt_copied, p0 + (m + 1))
                        if m >= 1:
                            pe.wait_ge(normed, p0 + m)
                        for g in range(HP):
                            ins = pe.matmul(o_ps[:, g, :, :].rearrange("p w d -> p (w d)"), pt[m % 2][:, g, :],
                                            v_bd[m % 8][:, g, :, :].rearrange("p w d -> p (w d)"),
                                            start=True, stop=True)
                        ins.then_inc(pv_done, 1)
                    if has(i - 3):
                        m = i - 3
                        pe.wait_ge(normed, p0 + (m + 1))
                        if m % 4 == 0 and m >= 4:
                            pe.wait_ge(xr_added, r0 + m // 4)
                        for w in range(2):
                            c0 = P * (m % 4) + TOK * w
                            ins = pe.matmul(ox_ps[:, c0:c0 + TOK], on[m % 2][:, w, :, :, :].rearrange(
                                "p a h d -> p (a h d)"), tokid[:, :], start=True, stop=True)
                        ins.then_inc(ot_done, 1)

                steps(pe, b, step)
                pe.wait_ge(xr_added, b * NROW + NROW)
                pe.wait_ge(ln_v, b * PAIRS + PAIRS)
                pe.wait_ge(biased, b * PAIRS + PAIRS)
                for t in range(T1N):
                    if t >= 4:
                        pe.wait_ge(gelu_done, b * T1N + (t - 3))
                    for a in range(4):
                        ay, ax = a // 2, a % 2
                        ins = pe.matmul(c_ps[t % 4][:, 0:T1R * (G + 1)], w1s[:, a, :],
                                        xr[:, T1R * t + ay:T1R * (t + 1) + ay, ax:ax + G + 1],
                                        start=(a == 0), stop=(a == 3))
                    ins.then_inc(c1_done, 1)
                pe.wait_ge(h_border, b + 1)
                for t in range(T2N):
                    if t >= 4:
                        pe.wait_ge(res_added, b * T2N + (t - 3) + 1)
                    for a in range(4):
                        ay, ax = a // 2, a % 2
                        ins = pe.matmul(c_ps[t % 4], w2s[:, a, :],
                                        hgrid[:, T2R * t + ay:T2R * (t + 1) + ay, ax:ax + G],
                                        start=(a == 0), stop=(a == 3))
                    ins.then_inc(c2_done, 1)


def _phases(n):
    p = np.arange(P)
    return p // (2 * C), p // C % 2, p % C


def _group_weights(w, e_out, shift):
    py, px, ci = _phases(P)
    oy, ox, co = e_out
    wp = np.zeros((P, 4, len(co)), w.dtype)
    for a in range(4):
        ky = (2 * (a // 2) + shift[0] * py[:, None] + shift[1] * oy[None, :] + shift[2]) + 0 * co[None, :]
        kx = (2 * (a % 2) + shift[0] * px[:, None] + shift[1] * ox[None, :] + shift[2]) + 0 * co[None, :]
        ok = (ky >= 0) & (ky < 3) & (kx >= 0) & (kx < 3)
        k, m = np.nonzero(ok)
        wp[k, a, m] = w[co[m], ci[k], ky[k, m], kx[k, m]]
    return wp


def kernel(**inputs):
    import concourse.bacc as _bacc
    from concourse.bass_utils import run_bass_kernel_spmd as _run

    arrays, outputs = _lay_out(inputs)
    nc = _bacc.Bacc("TRN2", target_bir_lowering=False, num_devices=1)
    args = {n: nc.dram_tensor(f"in_{n}_dram", a.shape, mybir.dt.from_np(a.dtype), kind="ExternalInput").ap()
            for n, a in arrays.items()}
    out = nc.dram_tensor("out_0_dram", (B, P, NT), F32, kind="ExternalOutput").ap()
    conv_attention(nc, out=out, **args)
    r = _run(nc, [{f"in_{n}_dram": a for n, a in arrays.items()}], core_ids=[0])
    y = r.results[0]["out_0_dram"].reshape(B, 2, 2, C, G, G)
    return np.ascontiguousarray(y.transpose(0, 3, 4, 1, 5, 2)).reshape(B, C, IMG, IMG)


def _lay_out(inputs):
    g = {k.replace("L0_conv_", ""): np.asarray(v) for k, v in inputs.items()}
    x = g["x"]
    xp = x.reshape(B, C, G, 2, G, 2).transpose(0, 3, 5, 1, 2, 4)
    x_al = np.ascontiguousarray(xp).reshape(B, P, NT)
    win = xp.reshape(B, 2, 2, C, NROW, TS, NWIN, TS)
    x_sh = np.zeros((B, 2, 2, C, NROW, NWIN, HALO, HALO), x.dtype)
    mask = np.zeros((2, 2, C, HALO, HALO), np.float32)
    for py in range(2):
        for px in range(2):
            x_sh[:, py, px, :, :, :, py:py + TS, px:px + TS] = win[:, py, px].transpose(0, 1, 2, 4, 3, 5)
            mask[py, px, :, py:py + TS, px:px + TS] = 1.0
    x_sh = x_sh.reshape(B, P, NROW, NWIN * HALO * HALO)
    mask = mask.reshape(P, HALO * HALO)

    e = np.arange(E)
    e_nat = (e // 2 % 2, e % 2, e // 4)
    order = [hp for bank in range(2) for hp in range(bank, HP, 2)]
    e_v = np.concatenate([e[2 * HD * hp:2 * HD * (hp + 1)] for hp in order])
    r_v = np.concatenate([e[HD * (2 * hp + par):HD * (2 * hp + par + 1)] for par in range(2) for hp in order])
    e_ph = _phases(P)
    e_m = e_ph[2] * 4 + e_ph[0] * 2 + e_ph[1]
    nat_v = tuple(a[e_v] for a in e_nat)
    wqkv = np.concatenate([_group_weights(g["qw"], e_nat, (-1, -1, 1)), _group_weights(g["kw"], e_nat, (-1, -1, 1)),
                           _group_weights(g["vw"], nat_v, (-1, -1, 1))], axis=2)
    bqkv = np.concatenate([g["qb"][e_nat[2]], g["kb"][e_nat[2]], g["vb"][nat_v[2]]])
    bqkv = np.ascontiguousarray(np.broadcast_to(bqkv, (P, QKV)))
    w1 = _group_weights(g["c1w"], e_ph, (1, 1, -1))
    w2 = _group_weights(g["c2w"], e_ph, (-1, -1, 1))
    pos = np.stack(np.meshgrid(np.arange(TS), np.arange(TS), indexing="ij")).reshape(2, -1)
    rel = pos[:, :, None] - pos[:, None, :] + TS - 1
    full = g["bias_table"][rel[0] * (2 * TS - 1) + rel[1]]
    bias_t = np.stack([full[:, :, [2 * hp + par for hp in order]] for par in range(2)])
    bias_t = np.broadcast_to(bias_t.transpose(0, 1, 3, 2)[:, :, :, None, :], (2, TOK, HP, 2, TOK))
    bias_t = np.ascontiguousarray(bias_t).reshape(P, 2, HP * TOK)
    proj_t = np.ascontiguousarray(g["proj_w"][e_m][:, r_v].T)
    even = (e // HD % 2 == 0).astype(np.float32)
    vecs = np.stack([g["gq"], g["bq"], g["gk"], g["bk"], even, 1 - even, g["gv"][r_v], g["bv"][r_v],
                     g["proj_b"][e_m], g["c1b"][e_ph[2]], g["c2b"][e_ph[2]]], axis=1)
    ident = np.eye(P, dtype=np.float32)
    sel_mean = (e[:, None] % C == e[None, :] % C).astype(np.float32) / 4
    sel_ones = np.zeros((P, P), np.float32)
    sel_ones[[0, 32, 64]] = 1.0
    tok_ident = np.tile(np.eye(TOK, dtype=np.float32), (2, 1))
    arrays = dict(x_al=x_al, x_sh=x_sh, mask=mask, wqkv=wqkv, bqkv=bqkv, bias_t=bias_t, proj_t=proj_t, vecs=vecs,
                  w1=w1, w2=w2, ident=ident, sel_mean=sel_mean, sel_ones=sel_ones, tok_ident=tok_ident)
    return {k: np.ascontiguousarray(v) for k, v in arrays.items()}, None
```

```python
from contextlib import ExitStack

import numpy as np

import concourse.bass as bass
from concourse import mybir

F32 = mybir.dt.float32
F16 = mybir.dt.float16
BF16 = mybir.dt.bfloat16
ALU = mybir.AluOpType
ACT = mybir.ActivationFunctionType
AX = mybir.AxisListType
RMAX = bass.bass_isa.ReduceOp.max

P = 128
B, C, IMG = 4, 32, 128
WIN = 16
TS = WIN // 2
TOK = TS * TS
E = 4 * C
HEADS = 8
HD = E // HEADS
HP = HEADS // 2
NROW = IMG // WIN
NWIN = IMG // WIN
PAIRS = NROW * NWIN // 2
G = IMG // 2
NT = G * G
HROWS = WIN + 2
HWIN = HROWS * TS
QKV = 3 * E
VW = 2 * HD + 1
GN_EPS = 1e-5
LN_EPS = 1e-5
SCALE = (C // HEADS) ** -0.5
XN_UP = 64.0
W_TOP = 16.0
QK_TOP = 8192.0
F16_TOP = 60000.0
LN_BOUND = float(E) ** 0.5
GN_BOUND = float(IMG)

GQ, BQ, GK, BK, GV, BV, PB, C1B, EVEN, ODD, C2B = range(11)
NVEC = 11

T1R = 5
T1N = (G + 1) // T1R
T2R = 8
T2N = G // T2R
NXF = 4


def conv_attention(nc, x_al, x_sh, mask, wqkv, bqkv, bias_t, proj_t, vecs, w1, w2, ident, sel_mean, sel_ones, tok_ident, out):
    with ExitStack() as ctx:
        def sb(name, shape, dt=F32):
            return ctx.enter_context(nc.sbuf_tensor(name, shape, dt))

        def psum(name, shape, dt=F32):
            return ctx.enter_context(nc.psum_tensor(name, shape, dt))

        def sem(name):
            return ctx.enter_context(nc.semaphore(name))

        y_ps = [psum(f"y_ps{i}", [P, 512]) for i in range(2)]
        t_ps = psum("t_ps", [P, 2, 2, P])
        s_ps = psum("s_ps", [P, 2, 512])
        pt_ps = psum("pt_ps", [P, HP, P])
        o_ps = psum("o_ps", [P, HP, 2, VW])
        ox_ps = psum("ox_ps", [P, 512])

        vec = sb("vec", [P, NVEC])
        idf = sb("idf", [P, P])
        selm = sb("selm", [P, P])
        tokid = sb("tokid", [P, TOK])
        maskt = sb("maskt", [P, HWIN])
        ones_f = sb("ones_f", [P, P])
        ones_b = sb("ones_b", [P, P], BF16)
        wst = sb("wst", [P, 4, QKV])
        w_hi = sb("w_hi", [P, 4, QKV], F16)
        w_lo = sb("w_lo", [P, 4, QKV], F16)
        bst = sb("bst", [P, QKV])
        b_parts = sb("b_parts", [P, QKV], BF16)
        b_tmp = sb("b_tmp", [P, QKV], BF16)
        biasS = sb("biasS", [P, 2, HP * TOK])
        projw = sb("projw", [P, P])
        projg = sb("projg", [P, P])
        w1s = sb("w1s", [P, 4, P])
        w2s = sb("w2s", [P, 4, P])
        w1_hi = sb("w1_hi", [P, 4, P], F16)
        w1_lo = sb("w1_lo", [P, 4, P], F16)
        w2_hi = sb("w2_hi", [P, 4, P], F16)
        w2_lo = sb("w2_lo", [P, 4, P], F16)
        A_VEC, A_PROJ, A_C1, A_C2 = 3, 11, 12, 13
        amax = sb("amax", [P, 14])
        amax_all = sb("amax_all", [P, 14])
        vb = sb("vb", [P, 2])
        bound = sb("bound", [P, 2])
        up = sb("up", [P, 2])
        wtop = sb("wtop", [P, 2])
        w_up = sb("w_up", [P, 2])
        y_up = sb("y_up", [P, 2])
        y_down = sb("y_down", [P, 2])
        c2_scale = sb("c2_scale", [P, 1])
        x_down = sb("x_down", [P, 1])
        cw = sb("cw", [P, 3])
        sw = sb("sw", [P, 3])
        eps_y = sb("eps_y", [P, 3])
        cqk = sb("cqk", [P, 4])
        qk_aff = sb("qk_aff", [P, 4])
        s_inv = sb("s_inv", [P, 1])
        neg_half = sb("neg_half", [P, 4])
        pbias = sb("pbias", [P, 1])
        wait_slot = sb("wait_slot", [P, 1])
        wait_exp = sb("wait_exp", [P, 1])

        xst = sb("xst", [P, NT])
        gst = sb("gst", [P, 8, 6])
        gmv = sb("gmv", [P, 2])
        gm = sb("gm", [P, 8])
        maskr = sb("maskr", [P, HWIN])
        xr = sb("xr", [P, G, G])
        xr_hi = sb("xr_hi", [P, G + 2, G + 2], F16)
        xr_lo = sb("xr_lo", [P, G + 2, G + 2], F16)
        hst = [sb(f"hst{i}", [P, T1R, G + 1]) for i in range(6)]
        h_hi = sb("h_hi", [P, G + 1, G + 1], F16)
        h_lo = sb("h_lo", [P, G + 1, G + 1], F16)
        xf = [sb(f"xf{i}", [P, 512]) for i in range(NXF)]
        yt = [sb(f"yt{i}", [P, 512]) for i in range(2)]

        xs = [sb(f"xs{i}", [P, NWIN, HWIN]) for i in range(2)]
        xnf = [sb(f"xnf{i}", [P, NWIN, HWIN]) for i in range(2)]
        x_hi = [sb(f"x_hi{i}", [P, 4, NWIN * TOK], F16) for i in range(2)]
        x_lo = [sb(f"x_lo{i}", [P, 4, NWIN * TOK], F16) for i in range(2)]
        ot = [sb(f"ot{i}", [P, 512]) for i in range(2)]

        ln_st = [sb(f"ln_st{i}", [P, 3, 6]) for i in range(2)]
        ln_mv = [sb(f"ln_mv{i}", [P, 3, 2]) for i in range(2)]
        ln_ve = [sb(f"ln_ve{i}", [P, 3]) for i in range(2)]
        ln_rs = [sb(f"ln_rs{i}", [P, 3]) for i in range(2)]
        ln_nm = [sb(f"ln_nm{i}", [P, 3]) for i in range(2)]
        ln_nr = [sb(f"ln_nr{i}", [P, 3]) for i in range(2)]
        qk_n = [sb(f"qk_n{i}", [P, 2, P]) for i in range(2)]
        v_bd = [sb(f"v_bd{i}", [P, HP, 2, VW]) for i in range(8)]
        sc = [sb(f"sc{i}", [P, HP, 2, TOK]) for i in range(4)]
        mx = [sb(f"mx{i}", [P, HP, 2]) for i in range(2)]
        pt = [sb(f"pt{i}", [P, HP, P]) for i in range(2)]
        rs = [sb(f"rs{i}", [P, HP, 2]) for i in range(2)]
        on = [sb(f"on{i}", [P, 2, 2, HP, HD]) for i in range(2)]
        qk_t = [sb(f"qk_t{i}", [P, 2, 2 * P]) for i in range(2)]
        q_hi = [sb(f"q_hi{i}", [P, 4, 2, TOK], F16) for i in range(2)]
        q_lo = [sb(f"q_lo{i}", [P, 4, 2, TOK], F16) for i in range(2)]
        k_hi = [sb(f"k_hi{i}", [P, 2 * P], F16) for i in range(2)]
        k_lo = [sb(f"k_lo{i}", [P, 2 * P], F16) for i in range(2)]

        loaded_qkv = sem("loaded_qkv")
        loaded_consts = sem("loaded_consts")
        zeroed = sem("zeroed")
        amax_done = sem("amax_done")
        w_scaled = sem("w_scaled")
        w_hi_done = sem("w_hi_done")
        c_scales = sem("c_scales")
        c_scaled = sem("c_scaled")
        c_hi_done = sem("c_hi_done")
        h_hi_done = sem("h_hi_done")
        h_split = sem("h_split")
        xr_hi_done = sem("xr_hi_done")
        xr_split = sem("xr_split")
        xf_biased = sem("xf_biased")
        setup_dve = sem("setup_dve")
        setup_pool = sem("setup_pool")
        setup_act = sem("setup_act")
        setup_pe = sem("setup_pe")
        weights_ready = sem("weights_ready")
        loaded_xst = sem("loaded_xst")
        loaded_xs = [sem(f"loaded_xs{i}") for i in range(2)]
        gn_chain = sem("gn_chain")
        gn_pe = sem("gn_pe")
        gn_dve = sem("gn_dve")
        gn_pool = sem("gn_pool")
        image_scaled = sem("image_scaled")
        xr_begun = sem("xr_begun")
        xn_done = sem("xn_done")
        xhi_done = sem("xhi_done")
        xlo_done = sem("xlo_done")
        conv_done = sem("conv_done")
        ln_stats = sem("ln_stats")
        ln_moments = sem("ln_moments")
        ln_var_eps = sem("ln_var_eps")
        ln_scales = sem("ln_scales")
        ln_qk = sem("ln_qk")
        ln_v = sem("ln_v")
        tr_done = sem("tr_done")
        qkt_done = sem("qkt_done")
        qk_hi_done = sem("qk_hi_done")
        qk_split = sem("qk_split")
        scores_done = sem("scores_done")
        biased = sem("biased")
        maxed = sem("maxed")
        shifted = sem("shifted")
        exped = sem("exped")
        ptr_done = sem("ptr_done")
        pt_copied = sem("pt_copied")
        pv_done = sem("pv_done")
        sums_inv = sem("sums_inv")
        normed = sem("normed")
        ot_done = sem("ot_done")
        ot_copied = sem("ot_copied")
        proj_done = sem("proj_done")
        xr_added = sem("xr_added")
        c1_done = sem("c1_done")
        gelu_done = sem("gelu_done")
        h_border = sem("h_border")
        c2_done = sem("c2_done")
        xf_loaded = [sem(f"xf_loaded{i}") for i in range(NXF)]
        res_added = sem("res_added")
        ln_pow = sem("ln_pow")
        h_rows = sem("h_rows")
        h_raw = sem("h_raw")
        scores_bank = sem("scores_bank")
        y_ready = sem("y_ready")
        stored = [sem(f"stored{i}") for i in range(NXF)]
        RES0 = 1
        BODY, BODIES = 8, 2
        HEAD = range(-4, 0)
        EPILOGUE = range(BODY * (1 + BODIES), PAIRS + 4)
        head_pair = [hp for bank in range(2) for hp in range(bank, HP, 2)]
        c_ps = [y_ps[0][:, :], y_ps[1][:, :], s_ps[:, 0, :], s_ps[:, 1, :]]

        def head(b, step, tile=None, tile_first=False):
            for i in HEAD:
                if tile is not None and tile_first:
                    tile(b - 1, T2N - len(HEAD) + HEAD.index(i))
                step(i, b * PAIRS, b * (PAIRS // 2), b * NROW, b * (NROW // 2), 0)
                if tile is not None and not tile_first:
                    tile(b - 1, T2N - len(HEAD) + HEAD.index(i))

        def steps(e, b, step, followed):
            for i in range(BODY):
                step(i, b * PAIRS, b * (PAIRS // 2), b * NROW, b * (NROW // 2), 0, b, followed)
            with e.Fori(0, BODIES) as t:
                for i in range(BODY, 2 * BODY):
                    step(i, b * PAIRS + t * BODY, b * (PAIRS // 2) + t * (BODY // 2), b * NROW + t * (BODY // 4),
                         b * (NROW // 2) + t * (BODY // 8), t * (BODY // 4), b, followed)
            for i in EPILOGUE:
                step(i, b * PAIRS, b * (PAIRS // 2), b * NROW, b * (NROW // 2), 0, b, followed)

        def at_offset(t, a):
            return t[:, a, :].rearrange("p (w i j) -> p w i j", w=NWIN, i=TS)

        def rows_under(t, a):
            g = t[:, :, :].rearrange("p w (i z j) -> p w i z j", z=2, j=TS)
            return g[:, :, a // 2:a // 2 + TS, a % 2, :]

        def by_head(y):
            return y.rearrange("p (y h x) -> p h y x", y=2, h=HEADS)

        c1_in = {28: (0,), 29: (1,), 30: (2,), 31: (3,), 32: (4, 5), 33: (6, 7), 34: (8,), 35: (9, 10)}
        c1_bank = [c_ps[t % 2 if t < 4 else (t + 2) % 4] for t in range(T1N)]
        c2_bank = [c_ps[k] for k in (3, 0, 1, 2, 3, 2, 3, 2)]
        split_in = {25: (0,), 26: (1,), 27: (2,), 28: (3,), 29: (4,), 30: (5,), 32: (6,)}
        low_in = {32: (0, 1, 2, 3), 33: (4, 5), 34: (6, 7), 35: (8,)}
        RAW1 = 4
        BORDER1 = 10
        parts_of = ((0,), (1,), (2, 3), ())

        def images(e, image):
            with e.Fori(0, B - 1) as b:
                image(b, True)
            image(B - 1, False)

        def has(n):
            return 0 <= n < PAIRS

        block = ctx.enter_context(nc.Block())

        @block.sync
        def _(sp):
            def load(dst, src, done):
                sp.dma_start(dst[tuple(slice(None) for _ in dst.shape)], src).then_inc(done, 16)

            for dst, src in ((vec, vecs), (wst, wqkv), (bst, bqkv), (ones_f, sel_ones)):
                load(dst, src, loaded_qkv)

            def row(b, r):
                if r >= 2:
                    sp.wait_ge(xn_done, b * NROW + r)
                else:
                    sp.wait_ge(xn_done, b * NROW + 1)
                sp.dma_start(xs[r % 2][:, :, :], x_sh[b, :, r, :].rearrange("p (w t) -> p w t", w=NWIN)).then_inc(
                    loaded_xs[r % 2], 16)

            def reload(b, t):
                sp.wait_ge(stored[t % NXF], (b * (T2N // NXF) + t // NXF + 1) * 16)
                sp.dma_start(xf[t % NXF][:, :], x_al[b, :, 512 * t:512 * (t + 1)]).then_inc(xf_loaded[t % NXF], 16)

            def image(b, followed):
                for r in range(4, NROW):
                    row(b, r)
                if followed:
                    sp.wait_ge(xr_begun, b * 4 + 5)
                    sp.dma_start(xst[:, :], x_al[b + 1]).then_inc(loaded_xst, 16)
                    row(b + 1, 0)
                    row(b + 1, 1)
                for t in range(NXF):
                    reload(b, t)
                if followed:
                    row(b + 1, 2)
                    row(b + 1, 3)
                for t in range(T2N):
                    sp.wait_ge(y_ready, b * T2N + (t + 1) + 1)
                    sp.dma_start(out[b, :, 512 * t:512 * (t + 1)], xf[t % NXF][:, :]).then_inc(stored[t % NXF], 16)
                    if 1 <= t < T2N - NXF + 1:
                        reload(b, t + NXF - 1)

            sp.dma_start(xst[:, :], x_al[0]).then_inc(loaded_xst, 16)
            for dst, src in ((selm, sel_mean), (maskt, mask), (projw, proj_t), (w1s, w1), (w2s, w2), (idf, ident),
                             (tokid, tok_ident), (biasS, bias_t)):
                load(dst, src, loaded_consts)
            for r in range(4):
                row(0, r)
            images(sp, image)
            for i in range(NXF):
                sp.wait_ge(stored[i], 16 * B * T2N // NXF + 16)

        @block.vector
        def _(v):
            n = [0]

            def link(ins):
                n[0] += 1
                ins.then_inc(setup_dve, 1)
                v.wait_ge(setup_dve, n[0])

            v.memset(neg_half[:, :], -0.5).then_inc(xr_begun, 1)
            v.memset(wait_slot[:, :], 0.0).then_inc(xn_done, 1)
            v.memset(s_inv[:, :], 0.0).then_inc(res_added, RES0)
            v.memset(pbias[:, :], 0.0).then_inc(y_ready, 1)
            v.memset(maskr[:, :], 0.0).then_inc(stored[0], 16)
            v.memset(gm[:, :], 0.0).then_inc(stored[1], 16)
            v.memset(w_up[:, :], 0.0).then_inc(stored[2], 16)
            v.memset(y_up[:, :], 0.0).then_inc(stored[3], 16)
            v.wait_ge(loaded_qkv, 16 * 4)
            for t in range(3):
                v.tensor_reduce(amax[:, t:t + 1], wst[:, :, E * t:E * (t + 1)], AX.XY, ALU.max,
                                apply_absolute_value=True)
            v.tensor_reduce(amax[:, A_VEC:A_PROJ], vec[:, 0:C1B + 1].unsqueeze(2), AX.X, ALU.max,
                            apply_absolute_value=True).then_inc(amax_done, 1)
            v.tensor_copy(ones_b[:, :], ones_f[:, :])
            v.wait_ge(setup_pool, 1)
            link(v.tensor_scalar(sw[:, :], amax_all[:, 0:3], 1e-15, None, ALU.max))
            link(v.reciprocal(cw[:, :], sw[:, :]))
            v.tensor_scalar(sw[:, :], cw[:, :], W_TOP, None, ALU.mult).then_inc(w_scaled, 1)
            v.wait_ge(w_scaled, 1)
            link(v.tensor_scalar(cw[:, :], sw[:, :], XN_UP, None, ALU.mult))
            for t in range(3):
                cols = slice(E * t, E * (t + 1))
                v.tensor_scalar(bst[:, cols], bst[:, cols], cw[:, t:t + 1], None, ALU.mult)
            link(v.tensor_tensor(eps_y[:, :], cw[:, :], cw[:, :], ALU.mult))
            gb = amax_all[:, A_VEC:A_VEC + 4].rearrange("p (j k) -> p j k", k=2)
            v.tensor_scalar(cqk[:, 0:2], gb[:, :, 0], LN_BOUND, 1e-15, ALU.mult, ALU.max)
            link(v.tensor_scalar(eps_y[:, :], eps_y[:, :], LN_EPS, None, ALU.mult))
            link(v.tensor_tensor(cqk[:, 2:4], cqk[:, 0:2], gb[:, :, 1], ALU.add))
            link(v.reciprocal(cqk[:, 0:2], cqk[:, 2:4]))
            v.tensor_tensor(s_inv[:, :], cqk[:, 2:3], cqk[:, 3:4], ALU.mult)
            link(v.tensor_scalar(cqk[:, 0:2], cqk[:, 0:2], QK_TOP, None, ALU.mult))
            v.tensor_scalar(s_inv[:, :], s_inv[:, :], SCALE / (QK_TOP * QK_TOP), None, ALU.mult)
            for j in range(2):
                v.tensor_scalar(qk_aff[:, 2 * j:2 * j + 2], vec[:, 2 * j:2 * j + 2], cqk[:, j:j + 1], None, ALU.mult)
            for t in range(3):
                cols = slice(E * t, E * (t + 1))
                v.wait_ge(w_hi_done, t + 1)
                v.scalar_tensor_tensor(w_lo[:, :, cols], wst[:, :, cols], sw[:, t:t + 1], w_hi[:, :, cols],
                                       ALU.mult, ALU.subtract)
            for j in range(3):
                link(v.tensor_copy(b_tmp[:, :], bst[:, :]))
                v.tensor_copy(b_parts[32 * j:32 * j + 32, :], b_tmp[32 * j:32 * j + 32, :])
                link(v.tensor_tensor(bst[:, :], bst[:, :], b_tmp[:, :], ALU.subtract))
            v.tensor_copy(wait_slot[:, :], vec[:, 0:1]).then_inc(weights_ready, 1)
            v.wait_ge(loaded_consts, 16 * 8)
            v.tensor_reduce(amax[:, A_PROJ:A_PROJ + 1], projw[:, :], AX.X, ALU.max, apply_absolute_value=True)
            v.tensor_reduce(amax[:, A_C1:A_C1 + 1], w1s[:, :, :], AX.XY, ALU.max, apply_absolute_value=True)
            v.tensor_reduce(amax[:, A_C2:A_C2 + 1], w2s[:, :, :], AX.XY, ALU.max, apply_absolute_value=True).then_inc(
                amax_done, 1)

            def conv_scales():
                v.wait_ge(setup_pool, 2)
                a_vec = lambda k: amax_all[:, A_VEC + k:A_VEC + k + 1]
                v.tensor_scalar(wtop[:, :], amax_all[:, A_C1:A_C2 + 1], 1e-15, None, ALU.max)
                link(v.scalar_tensor_tensor(vb[:, 0:1], a_vec(GV), LN_BOUND, a_vec(BV), ALU.mult, ALU.add))
                v.reciprocal(w_up[:, :], wtop[:, :])
                link(v.scalar_tensor_tensor(vb[:, 1:2], amax_all[:, A_PROJ:A_PROJ + 1], float(E), vb[:, 0:1],
                                            ALU.mult, ALU.mult))
                v.tensor_scalar(w_up[:, :], w_up[:, :], W_TOP, None, ALU.mult)
                link(v.scalar_tensor_tensor(bound[:, 0:1], vb[:, 1:2], GN_BOUND, a_vec(PB), ALU.add, ALU.add))
                link(v.tensor_scalar(bound[:, 1:2], bound[:, 0:1], wtop[:, 0:1], 9.0 * C, ALU.mult, ALU.mult))
                link(v.tensor_scalar(bound[:, 1:2], bound[:, 1:2], a_vec(C1B), 1e-10, ALU.add, ALU.max))
                link(v.reciprocal(up[:, :], bound[:, :]))
                link(v.tensor_scalar(up[:, :], up[:, :], F16_TOP, None, ALU.mult))
                v.tensor_scalar(x_down[:, :], bound[:, 0:1], 1.0 / F16_TOP, None, ALU.mult)
                link(v.tensor_tensor(y_up[:, :], up[:, :], w_up[:, :], ALU.mult))
                link(v.reciprocal(y_down[:, :], y_up[:, :]))
                v.tensor_scalar(projg[:, :], projw[:, :], vec[:, GV:GV + 1], up[:, 0:1], ALU.mult, ALU.mult)
                v.wait_ge(setup_pe, 1)
                v.tensor_scalar(pbias[:, :], ox_ps[:, 0:1], vec[:, PB:PB + 1], up[:, 0:1], ALU.add, ALU.mult)
                v.tensor_tensor(c2_scale[:, :], y_down[:, 1:2], up[:, 0:1], ALU.mult).then_inc(c_scales, 1)
                v.wait_ge(c_scales, 1)

            def stats(b, j):
                if j == 0:
                    v.wait_ge(loaded_xst, 16 * b + 16)
                ins = v.bn_stats(gst[:, j, :], xst[:, 512 * j:512 * (j + 1)])
                if j == 7:
                    ins.then_inc(gn_chain, 1)

            def moments(b):
                v.wait_ge(gn_chain, b * 6 + 1)
                v.tensor_copy(wait_slot[:, :], vec[:, 0:1])
                v.bn_aggr(gmv[:, :], gst[:, :, :]).then_inc(gn_dve, 1)

            def scales(b):
                v.wait_ge(gn_pe, b * 2 + 1)
                v.tensor_copy(gm[:, 0:1], ox_ps[:, 0:1]).then_inc(gn_chain, 1)
                v.wait_ge(gn_chain, b * 6 + 2)
                v.tensor_tensor(gm[:, 1:2], gmv[:, 0:1], gm[:, 0:1], ALU.subtract).then_inc(gn_chain, 1)
                v.wait_ge(gn_chain, b * 6 + 3)
                v.scalar_tensor_tensor(gm[:, 2:3], gm[:, 1:2], gm[:, 1:2], gmv[:, 1:2], ALU.mult, ALU.add).then_inc(
                    gn_dve, 1)
                v.wait_ge(gn_pe, b * 2 + 2)
                v.tensor_scalar(gm[:, 3:4], ox_ps[:, 0:1], GN_EPS, None, ALU.add).then_inc(gn_dve, 1)
                v.wait_ge(gn_pool, b + 1)
                v.tensor_scalar(maskr[:, :], maskt[:, :], gm[:, 4:5], XN_UP, ALU.mult, ALU.mult)
                v.tensor_tensor(gm[:, 7:8], gm[:, 4:5], up[:, 0:1], ALU.mult).then_inc(gn_chain, 1)
                v.wait_ge(gn_chain, b * 6 + 4)
                v.tensor_tensor(gm[:, 5:6], gm[:, 0:1], gm[:, 7:8], ALU.mult).then_inc(gn_chain, 1)
                v.wait_ge(gn_chain, b * 6 + 5)
                v.tensor_tensor(gm[:, 6:7], pbias[:, :], gm[:, 5:6], ALU.subtract).then_inc(gn_chain, 1)
                v.wait_ge(gn_chain, b * 6 + 6)

            def row(r, r0, rr0, first=False):
                v.wait_ge(loaded_xs[r % 2], (rr0 + (r // 2 + 1)) * 16)
                if not first:
                    v.wait_ge(xlo_done, (r0 + (r - 1)) * 4)
                v.scalar_tensor_tensor(
                    xnf[r % 2][:, :, :], xs[r % 2][:, :, :], gm[:, 0:1],
                    maskr[:, :].unsqueeze(1).to_broadcast([P, NWIN, HWIN]),
                    ALU.subtract, ALU.mult).then_inc(xn_done, 1)

            def low(b, t):
                rows = slice(T1R * t, T1R * (t + 1))
                v.wait_ge(gelu_done, b * T1N + (t + 1))
                v.tensor_scalar(h_hi[:, rows, :], hst[t % 6][:, :, :], up[:, 1:2], None, ALU.mult).then_inc(
                    h_hi_done, 1)
                v.wait_ge(h_hi_done, b * T1N + (t + 1))
                v.scalar_tensor_tensor(h_lo[:, rows, :], hst[t % 6][:, :, :], up[:, 1:2], h_hi[:, rows, :],
                                       ALU.mult, ALU.subtract).then_inc(h_split, 1)

            def border(b, done, zeros):
                v.wait_ge(h_split, b * T1N + done)
                for h in (h_hi, h_lo):
                    if done == T1N:
                        rows, edge = slice(T1R * BORDER1, G + 1), h[0:64, G:G + 1, :]
                    else:
                        rows, edge = slice(0, T1R * BORDER1), h[64:128, 0:1, :]
                    ins = v.memset(edge, 0.0)
                ins.then_inc(h_rows, 1)
                v.wait_ge(h_rows, b * 2 + zeros)
                for h in (h_hi, h_lo):
                    for q in range(4):
                        out_of = 0 if q % 2 else G
                        ins = v.memset(h[32 * q:32 * q + 32, rows, out_of:out_of + 1], 0.0)
                ins.then_inc(h_border, 1)

            def step(i, p0, h0, r0, rr0, row0, b=None, followed=False):
                if i % 4 == 0 and 2 <= (i + 8) // 4 < NROW:
                    row((i + 8) // 4, r0, rr0)
                if i % 2 == 1 and has(i + 1):
                    h = (i + 1) // 2
                    v.wait_ge(qkt_done, h0 + (h + 1))
                    if h >= 2:
                        v.wait_ge(scores_done, p0 + (2 * h - 2))
                    for par in range(2):
                        v.tensor_scalar(q_hi[h % 2][:, :, par, :],
                                        qk_t[h % 2][:, 0, :].rearrange("p (w t) -> p w t", w=4), vec[:, EVEN + par:EVEN + par + 1], None, ALU.mult)
                    v.tensor_copy(k_hi[h % 2][:, :], qk_t[h % 2][:, 1, :]).then_inc(qk_hi_done, 1)
                    v.wait_ge(qk_hi_done, h0 + (h + 1))
                    for par in range(2):
                        v.scalar_tensor_tensor(q_lo[h % 2][:, :, par, :],
                                               qk_t[h % 2][:, 0, :].rearrange("p (w t) -> p w t", w=4),
                                               vec[:, EVEN + par:EVEN + par + 1], q_hi[h % 2][:, :, par, :],
                                               ALU.mult, ALU.subtract)
                    v.tensor_tensor(k_lo[h % 2][:, :], qk_t[h % 2][:, 1, :], k_hi[h % 2][:, :],
                                    ALU.subtract).then_inc(qk_split, 1)
                if has(i + 4):
                    m = i + 4
                    v.wait_ge(conv_done, p0 + (m + 1))
                    if m >= 2:
                        v.wait_ge(ln_scales, p0 + (m - 1))
                    for t in range(3):
                        ins = v.bn_stats(ln_st[m % 2][:, t, :], y_ps[m % 2][:, E * t:E * (t + 1)])
                    ins.then_inc(ln_stats, 1)
                    v.wait_ge(ln_stats, p0 + (m + 1))
                    v.tensor_copy(wait_slot[:, :], vec[:, 0:1])
                    for t in range(3):
                        ins = v.bn_aggr(ln_mv[m % 2][:, t, :], ln_st[m % 2][:, t, :])
                    ins.then_inc(ln_moments, 1)
                if i % 4 == 3 and i >= 7:
                    r = (i - 7) // 4
                    v.wait_ge(proj_done, r0 + (r + 1))
                    if i == 7:
                        v.wait_ge(xr_begun, b * 4 + 5)
                    rows = xr[:, bass.ds((row0 + r) * TS, TS), :].rearrange("p i (w j) -> p w i j", w=NWIN)
                    v.tensor_tensor(rows, rows, ox_ps[:, :].rearrange("p (w i j) -> p w i j", w=NWIN, i=TS),
                                    ALU.add).then_inc(xr_added, 1)
                if has(i):
                    v.wait_ge(scores_done, p0 + (i + 1))
                    if i >= 4:
                        v.wait_ge(ptr_done, p0 + (i - 3))
                    v.scalar_tensor_tensor(sc[i % 4][:, :, :, :].rearrange("p (a h) w k -> p a (h w k)", a=2),
                                           s_ps[:, :, 0:256], s_inv[:, 0:1], biasS[:, :, :],
                                           ALU.mult, ALU.add).then_inc(biased, 1)
                    v.wait_ge(biased, p0 + (i + 1))
                    if i >= 2:
                        v.wait_ge(shifted, p0 + (i - 1))
                    v.tensor_reduce(mx[i % 2][:, :, :], sc[i % 4][:, :, :, :], AX.X, ALU.max).then_inc(maxed, 1)
                if has(i - 2):
                    m = i - 2
                    v.wait_ge(pv_done, p0 + (m + 1))
                    v.reciprocal(rs[m % 2][:, :, :], o_ps[:, :, :, VW - 1]).then_inc(sums_inv, 1)
                    v.wait_ge(sums_inv, p0 + (m + 1))
                    if m >= 2:
                        v.wait_ge(ot_done, p0 + (m - 1))
                    for par in range(2):
                        q = slice(64 * par, 64 * par + 64)
                        ins = v.tensor_tensor(
                            on[m % 2][q, :, par, :, :],
                            o_ps[q, :, :, HD * par:HD * (par + 1)].rearrange("p h w d -> p w h d"),
                            rs[m % 2][q, :, :].rearrange("p h w -> p w h").unsqueeze(3).to_broadcast(
                                [64, 2, HP, HD]),
                            ALU.mult)
                    ins.then_inc(normed, 1)
                if i >= PAIRS - 4 and followed:
                    stats(b + 1, i - (PAIRS - 4))
                for t in low_in.get(i, ()):
                    low(b, t)

            def result(b, t):
                v.wait_ge(c2_done, b * T2N + (t + 1))
                v.scalar_tensor_tensor(yt[t % 2][:, :], c2_bank[t], c2_scale[:, 0:1],
                                       xr[:, T2R * t:T2R * (t + 1), :].rearrange("p i j -> p (i j)"),
                                       ALU.mult, ALU.add).then_inc(res_added, 1)
                v.wait_ge(res_added, b * T2N + (t + 1) + RES0)
                v.wait_ge(xf_biased, b * T2N + (t + 1))
                v.scalar_tensor_tensor(xf[t % NXF][:, :], yt[t % 2][:, :], x_down[:, 0:1], xf[t % NXF][:, :],
                                       ALU.mult, ALU.add).then_inc(y_ready, 1)

            def image(b, followed):
                steps(v, b, step, followed)
                if followed:
                    moments(b + 1)
                low(b, 9)
                border(b, BORDER1, 1)
                if followed:
                    scales(b + 1)
                    row(0, (b + 1) * NROW, (b + 1) * (NROW // 2), first=False)
                    row(1, (b + 1) * NROW, (b + 1) * (NROW // 2), first=False)
                for t in range(BORDER1, T1N):
                    low(b, t)
                border(b, T1N, 2)
                for t in range(T2N - len(HEAD)):
                    result(b, t)
                if followed:
                    head(b + 1, step, result)
                else:
                    for t in range(T2N - len(HEAD), T2N):
                        result(b, t)

            conv_scales()
            for j in range(8):
                stats(0, j)
            moments(0)
            scales(0)
            row(0, 0, 0, first=True)
            row(1, 0, 0, first=True)
            head(0, step)
            images(v, image)

        @block.gpsimd
        def _(pool):
            for t in v_bd:
                pool.memset(t[:, :, :, :], 0.0)
            for t in on:
                pool.memset(t[:, :, :, :, :], 0.0)
            for t in (xr_hi, xr_lo):
                for k in (0, G + 1):
                    pool.memset(t[:, k:k + 1, :], 0.0)
                    ins = pool.memset(t[:, 1:G + 1, k:k + 1], 0.0)
            ins.then_inc(zeroed, 1)
            pool.wait_ge(zeroed, 1)
            for t in v_bd:
                pool.memset(t[0:64, :, 0, VW - 1:VW], 1.0)
                ins = pool.memset(t[64:128, :, 1, VW - 1:VW], 1.0)
            ins.then_inc(zeroed, 1)
            pool.wait_ge(zeroed, 2)
            pool.wait_ge(amax_done, 1)
            pool.partition_all_reduce(amax_all[:, 0:A_PROJ], amax[:, 0:A_PROJ], P, RMAX).then_inc(setup_pool, 1)
            pool.wait_ge(amax_done, 2)
            pool.partition_all_reduce(amax_all[:, A_PROJ:A_C2 + 1], amax[:, A_PROJ:A_C2 + 1], P, RMAX).then_inc(
                setup_pool, 1)
            pool.wait_ge(c_scales, 1)
            for j, w in enumerate((w1s, w2s)):
                pool.tensor_scalar(w[:, :, :], w[:, :, :], w_up[:, j:j + 1], None, ALU.mult).then_inc(c_scaled, 1)
            for j, (w, hi, lo) in enumerate(((w1s, w1_hi, w1_lo), (w2s, w2_hi, w2_lo))):
                pool.wait_ge(c_hi_done, j + 1)
                pool.tensor_tensor(lo[:, :, :], w[:, :, :], hi[:, :, :], ALU.subtract).then_inc(c_scaled, 1)

            def begin(b, first):
                pool.wait_ge(gn_dve, b * 3 + 3)
                pool.tensor_tensor(gm[:, 4:5], gm[:, 3:4], neg_half[:, 0:1], ALU.pow).then_inc(gn_pool, 1)
                for r in range(2):
                    for a in range(4):
                        part(r, a, b * PAIRS, b * NROW, first)

            def part(r, a, p0, r0, first=False):
                pool.wait_ge(xhi_done, (r0 + r) * 4 + a + 1)
                if r >= 2 or not first:
                    pool.wait_ge(conv_done, p0 + (4 * r - 4))
                pool.tensor_tensor(at_offset(x_lo[r % 2], a), rows_under(xnf[r % 2], a),
                                   at_offset(x_hi[r % 2], a), ALU.subtract).then_inc(xlo_done, 1)

            def split(b, r):
                pool.wait_ge(xr_hi_done, b * NROW + (r + 1))
                rows = slice(TS * r + 1, TS * (r + 1) + 1)
                pool.tensor_tensor(xr_lo[:, rows, 1:G + 1], xr[:, TS * r:TS * (r + 1), :], xr_hi[:, rows, 1:G + 1],
                                   ALU.subtract).then_inc(xr_split, 1)

            def step(i, p0, h0, r0, rr0, row0, b=None, followed=False):
                if has(i + 4):
                    m = i + 4
                    j = m % 2
                    pool.wait_ge(ln_moments, p0 + (m + 1))
                    if m >= 2:
                        pool.wait_ge(ln_v, p0 + (m - 1))
                    pool.tensor_tensor(ln_ve[j][:, :], ln_mv[j][:, :, 1], eps_y[:, :], ALU.add)
                    pool.tensor_scalar(ln_nm[j][:, :], ln_mv[j][:, :, 0], -1.0, None, ALU.mult).then_inc(
                        ln_var_eps, 1)
                    pool.wait_ge(ln_var_eps, p0 + (m + 1))
                    pool.tensor_tensor(ln_rs[j][:, :], ln_ve[j][:, :], neg_half[:, 0:3], ALU.pow).then_inc(
                        ln_pow, 1)
                    pool.wait_ge(ln_pow, p0 + (m + 1))
                    pool.tensor_tensor(ln_nr[j][:, :], ln_nm[j][:, :], ln_rs[j][:, :], ALU.mult).then_inc(
                        ln_scales, 1)
                if has(i):
                    pool.wait_ge(maxed, p0 + (i + 1))
                    pool.tensor_tensor(sc[i % 4][:, :, :, :], sc[i % 4][:, :, :, :],
                                       mx[i % 2][:, :, :].unsqueeze(3).to_broadcast([P, HP, 2, TOK]),
                                       ALU.subtract).then_inc(shifted, 1)
                if 2 <= (i + 8) // 4 < NROW:
                    for a in parts_of[i % 4]:
                        part((i + 8) // 4, a, p0, r0)
                for r in split_in.get(i, ()):
                    split(b, r)

            def image(b, followed):
                steps(pool, b, step, followed)
                split(b, NROW - 1)
                if followed:
                    begin(b + 1, False)
                    head(b + 1, step)

            begin(0, True)
            head(0, step)
            images(pool, image)

        @block.scalar
        def _(act):
            act.wait_ge(w_scaled, 1)
            for t in range(3):
                cols = slice(E * t, E * (t + 1))
                act.activation(w_hi[:, :, cols], wst[:, :, cols], ACT.Identity, scale=sw[:, t:t + 1]).then_inc(
                    w_hi_done, 1)
            for j, (w, hi) in enumerate(((w1s, w1_hi), (w2s, w2_hi))):
                act.wait_ge(c_scaled, j + 1)
                act.activation(hi[:, :, :], w[:, :, :], ACT.Copy).then_inc(c_hi_done, 1)
            act.wait_ge(zeroed, 2)

            def begin(b, first, r):
                for a in range(4):
                    part(r, a, b * PAIRS, b * NROW, first)

            def part(r, a, p0, r0, first=False):
                act.wait_ge(xn_done, r0 + (r + 1) + 1)
                if r >= 2 or not first:
                    act.wait_ge(conv_done, p0 + (4 * r - 4))
                act.activation(at_offset(x_hi[r % 2], a), rows_under(xnf[r % 2], a), ACT.Copy).then_inc(
                    xhi_done, 1)

            def gelu(b, t, src, **scaled):
                act.activation(hst[t % 6][:, :, :], src, ACT.Gelu, **scaled).then_inc(gelu_done, 1)

            def c1_tile(t):
                return c1_bank[t][:, 0:T1R * (G + 1)].rearrange("p (i j) -> p i j", i=T1R)

            def c1_out(b, t):
                act.wait_ge(c1_done, b * T1N + (t + 1))
                if t >= 6:
                    act.wait_ge(h_split, b * T1N + (t - 5))
                gelu(b, t, c1_tile(t), scale=y_down[:, 0:1], bias=vec[:, C1B:C1B + 1])

            def split(b, r):
                act.wait_ge(xr_added, b * NROW + (r + 1))
                act.activation(xr_hi[:, TS * r + 1:TS * (r + 1) + 1, 1:G + 1], xr[:, TS * r:TS * (r + 1), :],
                               ACT.Copy).then_inc(xr_hi_done, 1)

            def step(i, p0, h0, r0, rr0, row0, b=None, followed=False):
                if 2 <= (i + 8) // 4 < NROW:
                    for a in parts_of[i % 4]:
                        part((i + 8) // 4, a, p0, r0)
                if i % 2 == 0 and has(i + 2):
                    h = (i + 2) // 2
                    act.wait_ge(tr_done, p0 + (2 * h + 2))
                    if h >= 2:
                        act.wait_ge(qk_split, h0 + (h - 1))
                    for t in range(2):
                        ins = act.activation(qk_t[h % 2][:, t, :], t_ps[:, t, :, :].rearrange("p a n -> p (a n)"),
                                             ACT.Identity, scale=qk_aff[:, 2 * t:2 * t + 1],
                                             bias=qk_aff[:, 2 * t + 1:2 * t + 2])
                    ins.then_inc(qkt_done, 1)
                if has(i - 1):
                    m = i - 1
                    act.wait_ge(ptr_done, p0 + (m + 1))
                    if m >= 2:
                        act.wait_ge(pv_done, p0 + (m - 1))
                    act.activation(pt[m % 2][:, :, :], pt_ps[:, :, :], ACT.Copy).then_inc(pt_copied, 1)
                if i % 4 == 2 and i >= 6:
                    r = (i - 6) // 4
                    act.wait_ge(ot_done, p0 + (4 * r + 4))
                    if r >= 2:
                        act.wait_ge(proj_done, r0 + (r - 1))
                    act.activation(ot[r % 2][:, :], ox_ps[:, :], ACT.Copy).then_inc(ot_copied, 1)
                if has(i + 4):
                    m = i + 4
                    j = m % 2
                    act.wait_ge(ln_scales, p0 + (m + 1))
                    if m >= 2:
                        act.wait_ge(tr_done, p0 + (m - 1))
                    for t in range(2):
                        ins = act.activation(qk_n[j][:, t, :].rearrange("p (h y x) -> p h y x", h=HEADS, y=2),
                                             by_head(y_ps[j][:, E * t:E * (t + 1)]), ACT.Identity,
                                             scale=ln_rs[j][:, t:t + 1], bias=ln_nr[j][:, t:t + 1])
                    ins.then_inc(ln_qk, 1)
                    if m >= 8:
                        act.wait_ge(pv_done, p0 + (m - 7))
                    for w in range(2):
                        q = slice(64 * w, 64 * w + 64)
                        ins = act.activation(
                            v_bd[m % 8][q, :, w, 0:2 * HD].rearrange("p h (a y x) -> p h a y x", a=2, y=2),
                            y_ps[j][q, 2 * E:3 * E].rearrange("p (y h a x) -> p h a y x", y=2, h=HP, a=2),
                            ACT.Identity,
                            scale=ln_rs[j][q, 2:3], bias=ln_nr[j][q, 2:3])
                    ins.then_inc(ln_v, 1)
                if has(i):
                    act.wait_ge(shifted, p0 + (i + 1))
                    act.activation(sc[i % 4][:, :, :, :], sc[i % 4][:, :, :, :], ACT.Exp).then_inc(exped, 1)
                if i == PAIRS + 3:
                    split(b, NROW - 1)
                for t in c1_in.get(i, ()):
                    if t < RAW1:
                        act.wait_ge(c1_done, b * T1N + (t + 1))
                        act.activation(hst[t][:, :, :], c1_tile(t), ACT.Identity, scale=y_down[:, 0:1],
                                       bias=vec[:, C1B:C1B + 1]).then_inc(h_raw, 1)
                    else:
                        if t == RAW1:
                            act.wait_ge(h_raw, b * RAW1 + RAW1)
                            for u in range(RAW1):
                                gelu(b, u, hst[u][:, :, :])
                        c1_out(b, t)
                if 0 <= i < 4:
                    if i == 0:
                        act.wait_ge(res_added, b * T2N + RES0)
                    rows = slice(G // 4 * i, G // 4 * (i + 1))
                    act.activation(xr[:, rows, :].rearrange("p i j -> p (i j)"), xst[:, NT // 4 * i:NT // 4 * (i + 1)],
                                   ACT.Identity, scale=gm[:, 7:8], bias=gm[:, 6:7]).then_inc(xr_begun, 1)
                for r in split_in.get(i, ()):
                    split(b, r)

            def bias(b, t):
                act.wait_ge(xf_loaded[t % NXF], (b * (T2N // NXF) + (t // NXF + 1)) * 16)
                act.activation(xf[t % NXF][:, :], xf[t % NXF][:, :], ACT.Identity, bias=vec[:, C2B:C2B + 1]).then_inc(
                    xf_biased, 1)

            def image(b, followed):
                steps(act, b, step, followed)
                for t in range(11, T1N):
                    c1_out(b, t)
                for r in range(2):
                    if followed:
                        begin(b + 1, False, r)
                    for t in (2 * r, 2 * r + 1):
                        bias(b, t)
                act.activation(wait_exp[:, :], vec[:, 0:1], ACT.Exp)
                if followed:
                    head(b + 1, step, bias, tile_first=True)
                else:
                    for t in range(T2N - len(HEAD), T2N):
                        bias(b, t)

            begin(0, True, 0)
            begin(0, True, 1)
            act.activation(wait_exp[:, :], vec[:, 0:1], ACT.Exp)
            head(0, step)
            images(act, image)

        @block.tensor
        def _(pe):
            pe.wait_ge(loaded_consts, 16 * 8)
            pe.matmul(ox_ps[:, 0:1], projw[:, :], vec[:, BV:BV + 1], start=True, stop=True).then_inc(setup_pe, 1)
            pe.wait_ge(weights_ready, 1)
            pe.wait_ge(zeroed, 2)
            def mean_of_phases(b, n, of):
                pe.wait_ge(gn_dve, b * 3 + n)
                pe.matmul(ox_ps[:, 0:1], selm[:, :], of, start=True, stop=True).then_inc(gn_pe, 1)

            def c1(b, t):
                if t == 0:
                    pe.wait_ge(c_scaled, 4)
                pe.wait_ge(xr_split, b * NROW + min((T1R * (t + 1) - 1) // TS, NROW - 1) + 1)
                if t < 2:
                    pe.wait_ge(ln_v, b * PAIRS + PAIRS - 1 + t)
                elif t < RAW1:
                    pe.wait_ge(h_raw, b * RAW1 + (t - 1))
                elif t < 6:
                    pe.wait_ge(biased, b * PAIRS + PAIRS)
                elif t < 8:
                    pe.wait_ge(h_raw, b * RAW1 + (t - 3))
                else:
                    pe.wait_ge(gelu_done, b * T1N + (t - 3))
                for a in range(4):
                    ay, ax = a // 2, a % 2
                    for n, (ww, xx) in enumerate(((w1_hi, xr_hi), (w1_hi, xr_lo), (w1_lo, xr_hi))):
                        ins = pe.matmul(c1_bank[t][:, 0:T1R * (G + 1)], ww[:, a, :],
                                        xx[:, T1R * t + ay:T1R * (t + 1) + ay, ax:ax + G + 1],
                                        start=(a == 0 and n == 0), stop=(a == 3 and n == 2))
                ins.then_inc(c1_done, 1)

            def step(i, p0, h0, r0, rr0, row0, b=None, followed=False):
                if has(i + 4):
                    m = i + 4
                    r, s = m // 4, m % 4
                    if s == 0:
                        pe.wait_ge(xlo_done, (r0 + (r + 1)) * 4)
                    if m >= 2:
                        pe.wait_ge(ln_v, p0 + (m - 1))
                    y = y_ps[m % 2][:, 0:QKV]
                    pe.matmul(y, ones_b[0:96, :], b_parts[0:96, :], start=True, stop=False)
                    for a in range(4):
                        cols = {0: slice(0, E // 2), 3: slice(E // 2, E)}.get(a, slice(0, E))
                        for xx, ww in ((x_hi, w_hi), (x_hi, w_lo), (x_lo, w_hi)):
                            ins = pe.matmul(y.rearrange("p (t e) -> p t e", t=3)[:, :, cols],
                                            xx[r % 2][:, a, P * s:P * (s + 1)],
                                            ww[:, a, :].rearrange("p (t e) -> p t e", t=3)[:, :, cols],
                                            start=False, stop=(a == 3 and xx is x_lo))
                    ins.then_inc(conv_done, 1)
                if i < PAIRS + 3:
                    for t in c1_in.get(i, ()):
                        c1(b, t)
                if has(i + 3):
                    m = i + 3
                    pe.wait_ge(ln_qk, p0 + (m + 1))
                    if m % 2 == 0 and m >= 2:
                        pe.wait_ge(qkt_done, h0 + m // 2)
                    for t in range(2):
                        ins = pe.transpose(t_ps[:, t, m % 2, :], qk_n[m % 2][:, t, :], idf[:, :])
                    ins.then_inc(tr_done, 1)
                if i % 4 == 3 and i >= 7:
                    r = (i - 7) // 4
                    pe.wait_ge(ot_copied, r0 + (r + 1))
                    pe.matmul(ox_ps[:, :], projg[:, :], ot[r % 2][:, :], start=True, stop=True).then_inc(
                        proj_done, 1)
                if i == PAIRS + 3:
                    for t in c1_in[i]:
                        c1(b, t)
                if has(i):
                    h = i // 2
                    pe.wait_ge(qk_split, h0 + (h + 1))
                    if i == 0:
                        pe.wait_ge(res_added, b * T2N + RES0)
                    if i >= 1:
                        pe.wait_ge(biased, p0 + i)
                    for hp in range(HP):
                        rows = slice(32 * hp, 32 * hp + 32)
                        if hp >= 2:
                            pe.wait_ge(scores_bank, (p0 + i) * 2 + (hp - 1))
                        for w in range(2):
                            tok = slice(P * (i % 2) + TOK * w, P * (i % 2) + TOK * (w + 1))
                            c0 = (hp // 2) * 128 + TOK * w
                            for n, (qq, kk) in enumerate(((q_hi, k_hi), (q_hi, k_lo), (q_lo, k_hi))):
                                ins = pe.matmul(s_ps[:, hp % 2, c0:c0 + TOK], qq[h % 2][rows, 2 * (i % 2) + w, :, :].rearrange("p a t -> p (a t)"),
                                                kk[h % 2][rows, tok], start=(n == 0), stop=(n == 2))
                        if hp < 2:
                            ins.then_inc(scores_bank, 1)
                    ins.then_inc(scores_done, 1)
                if has(i - 1):
                    m = i - 1
                    pe.wait_ge(exped, p0 + (m + 1))
                    if m >= 1:
                        pe.wait_ge(pt_copied, p0 + m)
                    for g in range(HP):
                        ins = pe.transpose(pt_ps[:, g, :], sc[m % 4][:, g, :, :].rearrange("p w k -> p (w k)"),
                                           idf[:, :])
                    ins.then_inc(ptr_done, 1)
                if has(i - 2):
                    m = i - 2
                    pe.wait_ge(pt_copied, p0 + (m + 1))
                    if m >= 1:
                        pe.wait_ge(normed, p0 + m)
                    for g in range(HP):
                        ins = pe.matmul(o_ps[:, g, :, :].rearrange("p w d -> p (w d)"), pt[m % 2][:, g, :],
                                        v_bd[m % 8][:, g, :, :].rearrange("p w d -> p (w d)"),
                                        start=True, stop=True)
                    ins.then_inc(pv_done, 1)
                if has(i - 3):
                    m = i - 3
                    pe.wait_ge(normed, p0 + (m + 1))
                    if m % 4 == 0 and m >= 4:
                        pe.wait_ge(xr_added, r0 + m // 4)
                    for w in range(2):
                        c0 = P * (m % 4) + TOK * w
                        ins = pe.matmul(ox_ps[:, c0:c0 + TOK], on[m % 2][:, w, :, :, :].rearrange(
                            "p a h d -> p (a h d)"), tokid[:, :], start=True, stop=True)
                    ins.then_inc(ot_done, 1)

            def c2(b, t):
                if t == 0:
                    pe.wait_ge(h_border, b * 2 + 1)
                if T2R * (t + 1) + 1 > T1R * BORDER1:
                    pe.wait_ge(h_border, b * 2 + 2)
                if 1 <= t < 4:
                    pe.wait_ge(gelu_done, b * T1N + (10 + t))
                elif t >= 4:
                    pe.wait_ge(res_added, b * T2N + (1, 4, 5, 6)[t - 4] + RES0)
                for a in range(4):
                    ay, ax = a // 2, a % 2
                    for n, (ww, hh) in enumerate(((w2_hi, h_hi), (w2_hi, h_lo), (w2_lo, h_hi))):
                        ins = pe.matmul(c2_bank[t], ww[:, a, :],
                                        hh[:, T2R * t + ay:T2R * (t + 1) + ay, ax:ax + G],
                                        start=(a == 0 and n == 0), stop=(a == 3 and n == 2))
                ins.then_inc(c2_done, 1)

            def image(b, followed):
                steps(pe, b, step, followed)
                c1(b, 11)
                if followed:
                    mean_of_phases(b + 1, 1, gmv[:, 0:1])
                c1(b, 12)
                if followed:
                    mean_of_phases(b + 1, 2, gm[:, 2:3])
                for t in range(T2N - len(HEAD)):
                    c2(b, t)
                if followed:
                    pe.wait_ge(res_added, b * T2N + 3 + RES0)
                    head(b + 1, step, c2)
                else:
                    for t in range(T2N - len(HEAD), T2N):
                        c2(b, t)

            mean_of_phases(0, 1, gmv[:, 0:1])
            mean_of_phases(0, 2, gm[:, 2:3])
            head(0, step)
            images(pe, image)


def _phases(n):
    p = np.arange(P)
    return p // (2 * C), p // C % 2, p % C


def _group_weights(w, e_out, shift):
    py, px, ci = _phases(P)
    oy, ox, co = e_out
    wp = np.zeros((P, 4, len(co)), w.dtype)
    for a in range(4):
        ky = (2 * (a // 2) + shift[0] * py[:, None] + shift[1] * oy[None, :] + shift[2]) + 0 * co[None, :]
        kx = (2 * (a % 2) + shift[0] * px[:, None] + shift[1] * ox[None, :] + shift[2]) + 0 * co[None, :]
        ok = (ky >= 0) & (ky < 3) & (kx >= 0) & (kx < 3)
        k, m = np.nonzero(ok)
        wp[k, a, m] = w[co[m], ci[k], ky[k, m], kx[k, m]]
    return wp


def _row_weights(w, e_out):
    col, ci = np.divmod(np.arange(P), C)
    oy, ox, co = e_out
    wp = np.zeros((P, 4, len(co)), w.dtype)
    for a in range(4):
        ky = a - oy[None, :] + 0 * ci[:, None]
        kx = col[:, None] - ox[None, :]
        k, m = np.nonzero((ky >= 0) & (ky < 3) & (kx >= 0) & (kx < 3))
        wp[k, a, m] = w[co[m], ci[k], ky[k, m], kx[k, m]]
    return wp


def kernel(**inputs):
    import concourse.bacc as _bacc
    from concourse.bass_utils import run_bass_kernel_spmd as _run

    arrays, outputs = _lay_out(inputs)
    nc = _bacc.Bacc("TRN2", target_bir_lowering=False, num_devices=1)
    args = {n: nc.dram_tensor(f"in_{n}_dram", a.shape, mybir.dt.from_np(a.dtype), kind="ExternalInput").ap()
            for n, a in arrays.items()}
    out = nc.dram_tensor("out_0_dram", (B, P, NT), F32, kind="ExternalOutput").ap()
    conv_attention(nc, out=out, **args)
    r = _run(nc, [{f"in_{n}_dram": a for n, a in arrays.items()}], core_ids=[0])
    y = r.results[0]["out_0_dram"].reshape(B, 2, 2, C, G, G)
    return np.ascontiguousarray(y.transpose(0, 3, 4, 1, 5, 2)).reshape(B, C, IMG, IMG)


def _lay_out(inputs):
    g = {k.replace("L0_conv_", ""): np.asarray(v) for k, v in inputs.items()}
    x = g["x"]
    xp = x.reshape(B, C, G, 2, G, 2).transpose(0, 3, 5, 1, 2, 4)
    x_al = np.ascontiguousarray(xp).reshape(B, P, NT)
    win = np.zeros((B, C, NROW, NWIN, HROWS, HROWS), x.dtype)
    win[..., 1:-1, 1:-1] = x.reshape(B, C, NROW, WIN, NWIN, WIN).transpose(0, 1, 2, 4, 3, 5)
    inside = np.zeros((HROWS, HROWS), np.float32)
    inside[1:-1, 1:-1] = 1.0
    x_sh = np.stack([win[..., c:c + 2 * TS:2] for c in range(4)], axis=1).reshape(B, P, NROW, NWIN * HWIN)
    mask = np.repeat(np.stack([inside[:, c:c + 2 * TS:2] for c in range(4)]), C, axis=0).reshape(P, HWIN)

    e = np.arange(E)
    order = [hp for bank in range(2) for hp in range(bank, HP, 2)]
    hd, py, c4, px = np.unravel_index(e, (HEADS, 2, HD // 4, 2))
    f_nat = (hd * (HD // 4) + c4) * 4 + py * 2 + px
    py, hd, c4, px = np.unravel_index(e, (2, HEADS, HD // 4, 2))
    e_qk = (py, px, hd * (HD // 4) + c4)
    hd_v = 2 * np.array(order)[hd // 2] + hd % 2
    e_v = (py, px, hd_v * (HD // 4) + c4)
    r_v = np.concatenate([f_nat[HD * (2 * hp + par):HD * (2 * hp + par + 1)] for par in range(2) for hp in order])
    e_ph = _phases(P)
    e_m = e_ph[2] * 4 + e_ph[0] * 2 + e_ph[1]
    wqkv = np.concatenate([_row_weights(g["qw"], e_qk), _row_weights(g["kw"], e_qk), _row_weights(g["vw"], e_v)],
                          axis=2)
    bqkv = np.concatenate([g["qb"][e_qk[2]], g["kb"][e_qk[2]], g["vb"][e_v[2]]])
    bqkv = np.ascontiguousarray(np.broadcast_to(bqkv, (P, QKV)))
    w1 = _group_weights(g["c1w"], e_ph, (1, 1, -1))
    w2 = _group_weights(g["c2w"], e_ph, (-1, -1, 1))
    pos = np.stack(np.meshgrid(np.arange(TS), np.arange(TS), indexing="ij")).reshape(2, -1)
    rel = pos[:, :, None] - pos[:, None, :] + TS - 1
    full = g["bias_table"][rel[0] * (2 * TS - 1) + rel[1]]
    bias_t = np.stack([full[:, :, [2 * hp + par for hp in order]] for par in range(2)])
    bias_t = np.broadcast_to(bias_t.transpose(0, 1, 3, 2)[:, :, :, None, :], (2, TOK, HP, 2, TOK))
    bias_t = np.ascontiguousarray(bias_t).reshape(P, 2, HP * TOK)
    proj_t = np.ascontiguousarray(g["proj_w"][e_m][:, r_v].T)
    even = (e // HD % 2 == 0).astype(np.float32)
    vecs = np.stack([g["gq"][f_nat], g["bq"][f_nat], g["gk"][f_nat], g["bk"][f_nat], g["gv"][r_v], g["bv"][r_v],
                     g["proj_b"][e_m], g["c1b"][e_ph[2]], even, 1 - even, g["c2b"][e_ph[2]]], axis=1)
    ident = np.eye(P, dtype=np.float32)
    sel_mean = (e[:, None] % C == e[None, :] % C).astype(np.float32) / 4
    sel_ones = np.zeros((P, P), np.float32)
    sel_ones[[0, 32, 64]] = 1.0
    tok_ident = np.tile(np.eye(TOK, dtype=np.float32), (2, 1))
    arrays = dict(x_al=x_al, x_sh=x_sh, mask=mask, wqkv=wqkv, bqkv=bqkv, bias_t=bias_t, proj_t=proj_t, vecs=vecs,
                  w1=w1, w2=w2, ident=ident, sel_mean=sel_mean, sel_ones=sel_ones, tok_ident=tok_ident)
    return {k: np.ascontiguousarray(v) for k, v in arrays.items()}, None
```

```python
from contextlib import ExitStack

import numpy as np

import concourse.bass as bass
from concourse import mybir

F32 = mybir.dt.float32
F16 = mybir.dt.float16
BF16 = mybir.dt.bfloat16
ALU = mybir.AluOpType
ACT = mybir.ActivationFunctionType
AX = mybir.AxisListType
RMAX = bass.bass_isa.ReduceOp.max

P = 128
B, C, IMG = 4, 32, 128
WIN = 16
TS = WIN // 2
TOK = TS * TS
E = 4 * C
HEADS = 8
HD = E // HEADS
HP = HEADS // 2
NROW = IMG // WIN
NWIN = IMG // WIN
PAIRS = NROW * NWIN // 2
G = IMG // 2
NT = G * G
HROWS = WIN + 2
HWIN = HROWS * TS
QKV = 3 * E
VW = 2 * HD + 1
GN_EPS = 1e-5
LN_EPS = 1e-5
SCALE = (C // HEADS) ** -0.5
XN_UP = 64.0
W_TOP = 16.0
QK_TOP = 8192.0
F16_TOP = 60000.0
LN_BOUND = float(E) ** 0.5
GN_BOUND = float(IMG)

GQ, BQ, GK, BK, GV, BV, PB, C1B, EVEN, ODD, C2B = range(11)
NVEC = 11

T1R = 5
T1N = (G + 1) // T1R
T2R = 8
T2N = G // T2R
NXF = 4


def conv_attention(nc, x_al, x_sh, wqkv, bqkv, bias_t, proj_t, vecs, w1, w2, ident, sel_mean, sel_ones, out):
    with ExitStack() as ctx:
        def sb(name, shape, dt=F32):
            return ctx.enter_context(nc.sbuf_tensor(name, shape, dt))

        def psum(name, shape, dt=F32):
            return ctx.enter_context(nc.psum_tensor(name, shape, dt))

        def sem(name):
            return ctx.enter_context(nc.semaphore(name))

        y_ps = [psum(f"y_ps{i}", [P, 512]) for i in range(2)]
        t_ps = psum("t_ps", [P, 2, 2, P])
        s_ps = psum("s_ps", [P, 2, 512])
        pt_ps = psum("pt_ps", [P, HP, P])
        o_ps = psum("o_ps", [P, HP, 2, VW])
        ox_ps = psum("ox_ps", [P, 512])

        vec = sb("vec", [P, NVEC])
        idf = sb("idf", [P, P])
        selm = sb("selm", [P, P])
        ones_f = sb("ones_f", [P, P])
        ones_b = sb("ones_b", [P, P], BF16)
        wst = sb("wst", [P, 4, QKV])
        w_hi = sb("w_hi", [P, 4, QKV], F16)
        w_lo = sb("w_lo", [P, 4, QKV], F16)
        bst = sb("bst", [P, QKV])
        b_parts = sb("b_parts", [P, QKV], BF16)
        b_tmp = sb("b_tmp", [P, QKV], BF16)
        biasS = sb("biasS", [P, 2, HP * TOK])
        projw = sb("projw", [P, P])
        projg = sb("projg", [P, P])
        w1s = sb("w1s", [P, 4, P])
        w2s = sb("w2s", [P, 4, P])
        w1_hi = sb("w1_hi", [P, 4, P], F16)
        w1_lo = sb("w1_lo", [P, 4, P], F16)
        w2_hi = sb("w2_hi", [P, 4, P], F16)
        w2_lo = sb("w2_lo", [P, 4, P], F16)
        A_VEC, A_PROJ, A_C1, A_C2 = 3, 11, 12, 13
        amax = sb("amax", [P, 14])
        amax_all = sb("amax_all", [P, 14])
        vb = sb("vb", [P, 2])
        bound = sb("bound", [P, 2])
        up = sb("up", [P, 2])
        wtop = sb("wtop", [P, 2])
        w_up = sb("w_up", [P, 2])
        y_up = sb("y_up", [P, 2])
        y_down = sb("y_down", [P, 2])
        c2_scale = sb("c2_scale", [P, 1])
        x_down = sb("x_down", [P, 1])
        cw = sb("cw", [P, 3])
        sw = sb("sw", [P, 3])
        eps_y = sb("eps_y", [P, 3])
        cqk = sb("cqk", [P, 4])
        qk_aff = sb("qk_aff", [P, 4])
        s_inv = sb("s_inv", [P, 1])
        neg_half = sb("neg_half", [P, 4])
        pbias = sb("pbias", [P, 1])
        wait_slot = sb("wait_slot", [P, 1])
        wait_exp = sb("wait_exp", [P, 1])

        xst = sb("xst", [P, NT])
        gst = sb("gst", [P, 8, 6])
        gmv = sb("gmv", [P, 2])
        xn_aff = sb("xn_aff", [P, 2])
        gm = sb("gm", [P, 8])
        xr = sb("xr", [P, G, G])
        xr_hi = sb("xr_hi", [P, G + 2, G + 2], F16)
        xr_lo = sb("xr_lo", [P, G + 2, G + 2], F16)
        hst = [sb(f"hst{i}", [P, T1R, G + 1]) for i in range(6)]
        h_hi = sb("h_hi", [P, G + 1, G + 1], F16)
        h_lo = sb("h_lo", [P, G + 1, G + 1], F16)
        xf = [sb(f"xf{i}", [P, 512]) for i in range(NXF)]
        yt = [sb(f"yt{i}", [P, 512]) for i in range(2)]

        xs = [sb(f"xs{i}", [P, NWIN, HWIN]) for i in range(2)]
        xnf = [sb(f"xnf{i}", [P, NWIN, HWIN]) for i in range(2)]
        x_hi = [sb(f"x_hi{i}", [P, 4, NWIN * TOK], F16) for i in range(2)]
        x_lo = [sb(f"x_lo{i}", [P, 4, NWIN * TOK], F16) for i in range(2)]
        ot = [sb(f"ot{i}", [P, 512]) for i in range(2)]

        ln_st = [sb(f"ln_st{i}", [P, 3, 6]) for i in range(2)]
        ln_mv = [sb(f"ln_mv{i}", [P, 3, 2]) for i in range(2)]
        ln_ve = [sb(f"ln_ve{i}", [P, 3]) for i in range(2)]
        ln_rs = [sb(f"ln_rs{i}", [P, 3]) for i in range(2)]
        ln_nm = [sb(f"ln_nm{i}", [P, 3]) for i in range(2)]
        ln_nr = [sb(f"ln_nr{i}", [P, 3]) for i in range(2)]
        qk_n = [sb(f"qk_n{i}", [P, 2, P]) for i in range(2)]
        v_bd = [sb(f"v_bd{i}", [P, HP, 2, VW]) for i in range(8)]
        sc = [sb(f"sc{i}", [P, HP, 2, TOK]) for i in range(4)]
        mx = [sb(f"mx{i}", [P, HP, 2]) for i in range(2)]
        pt = [sb(f"pt{i}", [P, HP, P]) for i in range(2)]
        rs = [sb(f"rs{i}", [P, HP, 2]) for i in range(2)]
        on = [sb(f"on{i}", [P, 2, HP, HD]) for i in range(2)]
        qk_t = [sb(f"qk_t{i}", [P, 2, 2 * P]) for i in range(2)]
        q_hi = [sb(f"q_hi{i}", [P, 4, 2, TOK], F16) for i in range(2)]
        q_lo = [sb(f"q_lo{i}", [P, 4, 2, TOK], F16) for i in range(2)]
        k_hi = [sb(f"k_hi{i}", [P, 2 * P], F16) for i in range(2)]
        k_lo = [sb(f"k_lo{i}", [P, 2 * P], F16) for i in range(2)]

        loaded_qkv = sem("loaded_qkv")
        loaded_consts = sem("loaded_consts")
        zeroed = sem("zeroed")
        amax_done = sem("amax_done")
        w_scaled = sem("w_scaled")
        w_hi_done = sem("w_hi_done")
        c_scales = sem("c_scales")
        bias_scaled = sem("bias_scaled")
        bias_split = sem("bias_split")
        c_scaled = sem("c_scaled")
        c_hi_done = sem("c_hi_done")
        h_hi_done = sem("h_hi_done")
        h_split = sem("h_split")
        xr_hi_done = sem("xr_hi_done")
        xr_split = sem("xr_split")
        xf_biased = sem("xf_biased")
        setup_dve = sem("setup_dve")
        setup_pool = sem("setup_pool")
        setup_pe = sem("setup_pe")
        weights_ready = sem("weights_ready")
        loaded_xst = sem("loaded_xst")
        loaded_xs = [sem(f"loaded_xs{i}") for i in range(2)]
        gn_chain = sem("gn_chain")
        gn_pe = sem("gn_pe")
        gn_dve = sem("gn_dve")
        gn_pool = sem("gn_pool")
        xr_begun = sem("xr_begun")
        xn_scales = sem("xn_scales")
        xn_raw = sem("xn_raw")
        xn_done = sem("xn_done")
        xhi_done = sem("xhi_done")
        xlo_done = sem("xlo_done")
        conv_done = sem("conv_done")
        ln_stats = sem("ln_stats")
        ln_moments = sem("ln_moments")
        ln_var_eps = sem("ln_var_eps")
        ln_scales = sem("ln_scales")
        ln_qk = sem("ln_qk")
        ln_v = sem("ln_v")
        tr_done = sem("tr_done")
        qkt_done = sem("qkt_done")
        qk_hi_done = sem("qk_hi_done")
        qk_split = sem("qk_split")
        scores_done = sem("scores_done")
        biased = sem("biased")
        maxed = sem("maxed")
        shifted = sem("shifted")
        exped = sem("exped")
        ptr_done = sem("ptr_done")
        pt_copied = sem("pt_copied")
        pv_done = sem("pv_done")
        sums_inv = sem("sums_inv")
        normed = sem("normed")
        ot_done = sem("ot_done")
        ot_copied = sem("ot_copied")
        proj_done = sem("proj_done")
        xr_added = sem("xr_added")
        c1_done = sem("c1_done")
        gelu_done = sem("gelu_done")
        h_border = sem("h_border")
        c2_done = sem("c2_done")
        xf_loaded = [sem(f"xf_loaded{i}") for i in range(NXF)]
        res_added = sem("res_added")
        ln_pow = sem("ln_pow")
        h_rows = sem("h_rows")
        h_raw = sem("h_raw")
        scores_bank = sem("scores_bank")
        y_ready = sem("y_ready")
        stored = [sem(f"stored{i}") for i in range(NXF)]
        XR_FROM = 5
        RES0 = 1
        ADD0 = 1
        FIRST, BODY, BODIES = 4, 8, 2
        HEAD = range(-4, 0)
        EPILOGUE = range(FIRST + BODY * BODIES, PAIRS + 4)
        c_ps = [y_ps[0][:, :], y_ps[1][:, :], s_ps[:, 0, :], s_ps[:, 1, :]]

        def head(b, step, tile=None, tile_first=False):
            for i in HEAD:
                if tile is not None and tile_first:
                    tile(b - 1, T2N - len(HEAD) + HEAD.index(i))
                step(i, b * PAIRS, b * (PAIRS // 2), b * NROW, b * (NROW // 2), 0)
                if tile is not None and not tile_first:
                    tile(b - 1, T2N - len(HEAD) + HEAD.index(i))

        def steps(e, b, step, followed):
            for i in range(FIRST):
                step(i, b * PAIRS, b * (PAIRS // 2), b * NROW, b * (NROW // 2), 0, b, followed)
            with e.Fori(0, BODIES) as t:
                for i in range(FIRST, FIRST + BODY):
                    step(i, b * PAIRS + t * BODY, b * (PAIRS // 2) + t * (BODY // 2), b * NROW + t * (BODY // 4),
                         b * (NROW // 2) + t * (BODY // 8), t * (BODY // 4), b, followed)
            for i in EPILOGUE:
                step(i, b * PAIRS, b * (PAIRS // 2), b * NROW, b * (NROW // 2), 0, b, followed)

        def inner(a):
            return slice(1, TS) if a == 0 else slice(0, TS - 1) if a == 3 else slice(0, TS)

        def at_offset(t, a):
            return t[:, a, :].rearrange("p (w i j) -> p w i j", w=NWIN, i=TS)[:, :, inner(a), :]

        def rows_under(t, a):
            g = t[:, :, :].rearrange("p w (i z j) -> p w i z j", z=2, j=TS)
            return g[:, :, a // 2 + inner(a).start:a // 2 + inner(a).stop, a % 2, :]

        def by_head(y):
            return y.rearrange("p (y h x) -> p h y x", y=2, h=HEADS)

        c1_in = {28: (0,), 29: (1,), 30: (2,), 31: (3,), 32: (4, 5), 33: (6, 7), 34: (8,), 35: (9, 10)}
        c1_bank = [c_ps[t % 2 if t < 4 else (t + 2) % 4] for t in range(T1N)]
        c2_bank = [c_ps[k] for k in (3, 0, 1, 2, 3, 2, 3, 2)]
        split_in = {25: (0,), 26: (1,), 27: (2,), 28: (3,), 29: (4,), 30: (5,), 32: (6,)}
        low_in = {32: (0, 1, 2, 3), 33: (4, 5), 35: (6, 7, 8)}
        RAW1 = 4
        BORDER1 = 10
        parts_of = ((0,), (1, 2), (3,), ())

        def images(e, image):
            with e.Fori(0, B - 1) as b:
                image(b, True)
            image(B - 1, False)

        def has(n):
            return 0 <= n < PAIRS

        block = ctx.enter_context(nc.Block())

        @block.sync
        def _(sp):
            def load(dst, src, done):
                sp.dma_start(dst[tuple(slice(None) for _ in dst.shape)], src).then_inc(done, 16)

            for dst, src in ((vec, vecs), (wst, wqkv), (bst, bqkv), (ones_f, sel_ones)):
                load(dst, src, loaded_qkv)

            def row(b, r):
                if r >= 2:
                    sp.wait_ge(xn_done, b * NROW + r)
                else:
                    sp.wait_ge(xn_done, b * NROW + 1)
                sp.dma_start(xs[r % 2][:, :, :], x_sh[b, :, r, :].rearrange("p (w t) -> p w t", w=NWIN)).then_inc(
                    loaded_xs[r % 2], 16)

            def reload(b, t):
                sp.wait_ge(stored[t % NXF], (b * (T2N // NXF) + t // NXF + 1) * 16)
                sp.dma_start(xf[t % NXF][:, :], x_al[b, :, 512 * t:512 * (t + 1)]).then_inc(xf_loaded[t % NXF], 16)

            def image(b, followed):
                for r in range(4, NROW):
                    row(b, r)
                if followed:
                    sp.wait_ge(xr_begun, b * 4 + 5)
                    sp.dma_start(xst[:, :], x_al[b + 1]).then_inc(loaded_xst, 16)
                    row(b + 1, 0)
                    row(b + 1, 1)
                for t in range(NXF):
                    reload(b, t)
                if followed:
                    row(b + 1, 2)
                    row(b + 1, 3)
                for t in range(T2N):
                    sp.wait_ge(y_ready, b * T2N + (t + 1) + 1)
                    sp.dma_start(out[b, :, 512 * t:512 * (t + 1)], xf[t % NXF][:, :]).then_inc(stored[t % NXF], 16)
                    if 1 <= t < T2N - NXF + 1:
                        reload(b, t + NXF - 1)

            sp.dma_start(xst[:, :], x_al[0]).then_inc(loaded_xst, 16)
            for dst, src in ((selm, sel_mean), (projw, proj_t), (w1s, w1), (w2s, w2), (idf, ident),
                             (biasS, bias_t)):
                load(dst, src, loaded_consts)
            for r in range(4):
                row(0, r)
            images(sp, image)
            for i in range(NXF):
                sp.wait_ge(stored[i], 16 * B * T2N // NXF + 16)

        @block.vector
        def _(v):
            n = [0]

            def link(ins):
                n[0] += 1
                ins.then_inc(setup_dve, 1)
                v.wait_ge(setup_dve, n[0])

            v.memset(neg_half[:, :], -0.5).then_inc(xr_begun, 1)
            v.memset(wait_slot[:, :], 0.0).then_inc(xn_done, 1)
            v.memset(s_inv[:, :], 0.0).then_inc(res_added, RES0)
            v.memset(xn_aff[:, :], 0.0).then_inc(xr_added, ADD0)
            v.memset(pbias[:, :], 0.0).then_inc(y_ready, 1)
            v.memset(up[:, :], 0.0).then_inc(stored[0], 16)
            v.memset(gm[:, :], 0.0).then_inc(stored[1], 16)
            v.memset(w_up[:, :], 0.0).then_inc(stored[2], 16)
            v.memset(y_up[:, :], 0.0).then_inc(stored[3], 16)
            v.wait_ge(loaded_qkv, 16 * 4)
            for t in range(3):
                v.tensor_reduce(amax[:, t:t + 1], wst[:, :, E * t:E * (t + 1)], AX.XY, ALU.max,
                                apply_absolute_value=True)
            v.tensor_reduce(amax[:, A_VEC:A_PROJ], vec[:, 0:C1B + 1].unsqueeze(2), AX.X, ALU.max,
                            apply_absolute_value=True).then_inc(amax_done, 1)
            v.tensor_copy(ones_b[:, :], ones_f[:, :])
            v.wait_ge(setup_pool, 1)
            link(v.tensor_scalar(sw[:, :], amax_all[:, 0:3], 1e-15, None, ALU.max))
            link(v.reciprocal(cw[:, :], sw[:, :]))
            v.tensor_scalar(sw[:, :], cw[:, :], W_TOP, None, ALU.mult).then_inc(w_scaled, 1)
            v.wait_ge(w_scaled, 1)
            link(v.tensor_scalar(cw[:, :], sw[:, :], XN_UP, None, ALU.mult))
            for t in range(3):
                cols = slice(E * t, E * (t + 1))
                v.tensor_scalar(bst[:, cols], bst[:, cols], cw[:, t:t + 1], None, ALU.mult).then_inc(bias_scaled, 1)
            link(v.tensor_tensor(eps_y[:, :], cw[:, :], cw[:, :], ALU.mult))
            def low_weights():
                for t in range(3):
                    cols = slice(E * t, E * (t + 1))
                    v.wait_ge(w_hi_done, t + 1)
                    v.scalar_tensor_tensor(w_lo[:, :, cols], wst[:, :, cols], sw[:, t:t + 1], w_hi[:, :, cols],
                                           ALU.mult, ALU.subtract).then_inc(weights_ready, 1)

            def qk_scales():
                gb = amax_all[:, A_VEC:A_VEC + 4].rearrange("p (j k) -> p j k", k=2)
                v.tensor_scalar(cqk[:, 0:2], gb[:, :, 0], LN_BOUND, 1e-15, ALU.mult, ALU.max)
                link(v.tensor_scalar(eps_y[:, :], eps_y[:, :], LN_EPS, None, ALU.mult))
                link(v.tensor_tensor(cqk[:, 2:4], cqk[:, 0:2], gb[:, :, 1], ALU.add))
                link(v.reciprocal(cqk[:, 0:2], cqk[:, 2:4]))
                v.tensor_tensor(s_inv[:, :], cqk[:, 2:3], cqk[:, 3:4], ALU.mult)
                link(v.tensor_scalar(cqk[:, 0:2], cqk[:, 0:2], QK_TOP, None, ALU.mult))
                v.tensor_scalar(s_inv[:, :], s_inv[:, :], SCALE / (QK_TOP * QK_TOP), None, ALU.mult)
                for j in range(2):
                    v.tensor_scalar(qk_aff[:, 2 * j:2 * j + 2], vec[:, 2 * j:2 * j + 2], cqk[:, j:j + 1], None, ALU.mult)

            def largest():
                v.wait_ge(loaded_consts, 16 * 6)
                v.tensor_reduce(amax[:, A_PROJ:A_PROJ + 1], projw[:, :], AX.X, ALU.max, apply_absolute_value=True)
                v.tensor_reduce(amax[:, A_C1:A_C1 + 1], w1s[:, :, :], AX.XY, ALU.max, apply_absolute_value=True)
                v.tensor_reduce(amax[:, A_C2:A_C2 + 1], w2s[:, :, :], AX.XY, ALU.max, apply_absolute_value=True).then_inc(
                    amax_done, 1)

            def conv_scales():
                v.wait_ge(setup_pool, 2)
                a_vec = lambda k: amax_all[:, A_VEC + k:A_VEC + k + 1]
                v.tensor_scalar(wtop[:, :], amax_all[:, A_C1:A_C2 + 1], 1e-15, None, ALU.max)
                link(v.scalar_tensor_tensor(vb[:, 0:1], a_vec(GV), LN_BOUND, a_vec(BV), ALU.mult, ALU.add))
                v.reciprocal(w_up[:, :], wtop[:, :])
                link(v.scalar_tensor_tensor(vb[:, 1:2], amax_all[:, A_PROJ:A_PROJ + 1], float(E), vb[:, 0:1],
                                            ALU.mult, ALU.mult))
                v.tensor_scalar(w_up[:, :], w_up[:, :], W_TOP, None, ALU.mult)
                link(v.scalar_tensor_tensor(bound[:, 0:1], vb[:, 1:2], GN_BOUND, a_vec(PB), ALU.add, ALU.add))
                link(v.tensor_scalar(bound[:, 1:2], bound[:, 0:1], wtop[:, 0:1], 9.0 * C, ALU.mult, ALU.mult))
                link(v.tensor_scalar(bound[:, 1:2], bound[:, 1:2], a_vec(C1B), 1e-10, ALU.add, ALU.max))
                link(v.reciprocal(up[:, :], bound[:, :]))
                link(v.tensor_scalar(up[:, :], up[:, :], F16_TOP, None, ALU.mult))
                v.tensor_scalar(x_down[:, :], bound[:, 0:1], 1.0 / F16_TOP, None, ALU.mult)
                link(v.tensor_tensor(y_up[:, :], up[:, :], w_up[:, :], ALU.mult))
                link(v.reciprocal(y_down[:, :], y_up[:, :]))
                v.tensor_scalar(projg[:, :], projw[:, :], vec[:, GV:GV + 1], up[:, 0:1], ALU.mult, ALU.mult)
                v.wait_ge(setup_pe, 1)
                v.tensor_scalar(pbias[:, :], pt_ps[:, 0, 0:1], vec[:, PB:PB + 1], up[:, 0:1], ALU.add, ALU.mult)
                v.tensor_tensor(c2_scale[:, :], y_down[:, 1:2], up[:, 0:1], ALU.mult).then_inc(c_scales, 1)
                v.wait_ge(c_scales, 1)

            def low_conv_weights():
                for j, (w, hi, lo) in enumerate(((w1s, w1_hi, w1_lo), (w2s, w2_hi, w2_lo))):
                    v.wait_ge(c_hi_done, j + 1)
                    v.scalar_tensor_tensor(lo[:, :, :], w[:, :, :], w_up[:, j:j + 1], hi[:, :, :], ALU.mult,
                                           ALU.subtract).then_inc(c_scaled, 1)

            def stats(b, j):
                if j == 0:
                    v.wait_ge(loaded_xst, 16 * b + 16)
                ins = v.bn_stats(gst[:, j, :], xst[:, 512 * j:512 * (j + 1)])
                if j == 7:
                    ins.then_inc(gn_chain, 1)

            def moments(b):
                v.wait_ge(gn_chain, b * 7 + 1)
                v.tensor_copy(wait_slot[:, :], vec[:, 0:1])
                v.bn_aggr(gmv[:, :], gst[:, :, :]).then_inc(gn_dve, 1)

            def scales(b, meanwhile=None):
                v.wait_ge(gn_pe, b * 2 + 1)
                v.tensor_copy(gm[:, 0:1], ox_ps[:, 0:1]).then_inc(gn_chain, 1)
                v.wait_ge(gn_chain, b * 7 + 2)
                v.tensor_tensor(gm[:, 1:2], gmv[:, 0:1], gm[:, 0:1], ALU.subtract).then_inc(gn_chain, 1)
                v.wait_ge(gn_chain, b * 7 + 3)
                v.scalar_tensor_tensor(gm[:, 2:3], gm[:, 1:2], gm[:, 1:2], gmv[:, 1:2], ALU.mult, ALU.add).then_inc(
                    gn_dve, 1)
                v.wait_ge(gn_pe, b * 2 + 2)
                v.tensor_scalar(gm[:, 3:4], ox_ps[:, 0:1], GN_EPS, None, ALU.add).then_inc(gn_dve, 1)
                if meanwhile is not None:
                    meanwhile()
                v.wait_ge(gn_pool, b + 1)
                v.tensor_scalar(xn_aff[:, 0:1], gm[:, 4:5], XN_UP, None, ALU.mult).then_inc(gn_chain, 1)
                v.wait_ge(gn_chain, b * 7 + 4)
                v.scalar_tensor_tensor(xn_aff[:, 1:2], gm[:, 0:1], -1.0, xn_aff[:, 0:1], ALU.mult, ALU.mult).then_inc(
                    xn_scales, 1)

            def start_scales(b):
                v.tensor_tensor(gm[:, 7:8], gm[:, 4:5], up[:, 0:1], ALU.mult).then_inc(gn_chain, 1)
                v.wait_ge(gn_chain, b * 7 + 5)
                v.tensor_tensor(gm[:, 5:6], gm[:, 0:1], gm[:, 7:8], ALU.mult).then_inc(gn_chain, 1)
                v.wait_ge(gn_chain, b * 7 + 6)
                v.tensor_tensor(gm[:, 6:7], pbias[:, :], gm[:, 5:6], ALU.subtract).then_inc(gn_chain, 1)
                v.wait_ge(gn_chain, b * 7 + 7)

            def row(r, r0):
                v.wait_ge(xn_raw, r0 + (r + 1))
                t = xnf[r % 2][:, :, :].rearrange("p w (i j) -> p w i j", j=TS)
                v.memset(t[0:C, :, 1:HROWS - 1, 0:1], 0.0)
                v.memset(t[3 * C:4 * C, :, 1:HROWS - 1, TS - 1:TS], 0.0).then_inc(xn_done, 1)

            def low(b, t):
                rows = slice(T1R * t, T1R * (t + 1))
                v.wait_ge(gelu_done, b * T1N + (t + 1))
                v.tensor_scalar(h_hi[:, rows, :], hst[t % 6][:, :, :], up[:, 1:2], None, ALU.mult).then_inc(
                    h_hi_done, 1)
                v.wait_ge(h_hi_done, b * T1N + (t + 1))
                v.scalar_tensor_tensor(h_lo[:, rows, :], hst[t % 6][:, :, :], up[:, 1:2], h_hi[:, rows, :],
                                       ALU.mult, ALU.subtract).then_inc(h_split, 1)

            def border(b, done, zeros):
                v.wait_ge(h_split, b * T1N + done)
                for h in (h_hi, h_lo):
                    if done == T1N:
                        rows, edge = slice(T1R * BORDER1, G + 1), h[0:64, G:G + 1, :]
                    else:
                        rows, edge = slice(0, T1R * BORDER1), h[64:128, 0:1, :]
                    ins = v.memset(edge, 0.0)
                ins.then_inc(h_rows, 1)
                v.wait_ge(h_rows, b * 2 + zeros)
                for h in (h_hi, h_lo):
                    for q in range(4):
                        out_of = 0 if q % 2 else G
                        ins = v.memset(h[32 * q:32 * q + 32, rows, out_of:out_of + 1], 0.0)
                ins.then_inc(h_border, 1)

            def low_qk(i, h0):
                if has(i + 1):
                    h = (i + 1) // 2
                    v.wait_ge(qk_hi_done, h0 + (h + 1))
                    for par in range(2):
                        v.scalar_tensor_tensor(q_lo[h % 2][:, :, par, :],
                                               qk_t[h % 2][:, 0, :].rearrange("p (w t) -> p w t", w=4),
                                               vec[:, EVEN + par:EVEN + par + 1], q_hi[h % 2][:, :, par, :],
                                               ALU.mult, ALU.subtract)
                    v.tensor_tensor(k_lo[h % 2][:, :], qk_t[h % 2][:, 1, :], k_hi[h % 2][:, :],
                                    ALU.subtract).then_inc(qk_split, 1)

            def step(i, p0, h0, r0, rr0, row0, b=None, followed=False):
                if has(i + 4):
                    m = i + 4
                    v.wait_ge(conv_done, p0 + (m + 1))
                    if m >= 2:
                        v.wait_ge(ln_scales, p0 + (m - 1))
                    for t in range(3):
                        ins = v.bn_stats(ln_st[m % 2][:, t, :], y_ps[m % 2][:, E * t:E * (t + 1)])
                    ins.then_inc(ln_stats, 1)
                    v.wait_ge(ln_stats, p0 + (m + 1))
                    v.tensor_copy(wait_slot[:, :], vec[:, 0:1])
                    for t in range(3):
                        ins = v.bn_aggr(ln_mv[m % 2][:, t, :], ln_st[m % 2][:, t, :])
                    ins.then_inc(ln_moments, 1)
                if i % 4 == 3:
                    low_qk(i, h0)
                if has(i):
                    v.wait_ge(scores_done, p0 + (i + 1))
                    if i >= 4:
                        v.wait_ge(ptr_done, p0 + (i - 3))
                    v.scalar_tensor_tensor(sc[i % 4][:, :, :, :].rearrange("p (a h) w k -> p a (h w k)", a=2),
                                           s_ps[:, :, 0:256], s_inv[:, 0:1], biasS[:, :, :],
                                           ALU.mult, ALU.add).then_inc(biased, 1)
                if i % 4 == 3 and i >= 7:
                    r = (i - 7) // 4
                    v.wait_ge(proj_done, r0 + (r + 1))
                    if i == 7:
                        v.wait_ge(xr_begun, b * 4 + 5)
                    rows = xr[:, bass.ds((row0 + r) * TS, TS), :].rearrange("p i (w j) -> p w i j", w=NWIN)
                    v.tensor_tensor(rows, rows, ox_ps[:, :].rearrange("p (w i j) -> p w i j", w=NWIN, i=TS),
                                    ALU.add).then_inc(xr_added, 1)
                if has(i):
                    v.wait_ge(biased, p0 + (i + 1))
                    if i >= 2:
                        v.wait_ge(shifted, p0 + (i - 1))
                    v.tensor_reduce(mx[i % 2][:, :, :], sc[i % 4][:, :, :, :], AX.X, ALU.max).then_inc(maxed, 1)
                if i % 4 == 1:
                    low_qk(i, h0)
                if i % 4 == 3 and 2 <= (i + 9) // 4 < NROW:
                    row((i + 9) // 4, r0)
                if has(i - 2):
                    m = i - 2
                    v.wait_ge(pv_done, p0 + (m + 1))
                    v.reciprocal(rs[m % 2][:, :, :], o_ps[:, :, :, VW - 1]).then_inc(sums_inv, 1)
                    v.wait_ge(sums_inv, p0 + (m + 1))
                    if m >= 2:
                        v.wait_ge(ot_done, p0 + (m - 1))
                    for par in range(2):
                        q = slice(64 * par, 64 * par + 64)
                        ins = v.tensor_tensor(
                            on[m % 2][q, :, :, :],
                            o_ps[q, :, :, HD * par:HD * (par + 1)].rearrange("p h w d -> p w h d"),
                            rs[m % 2][q, :, :].rearrange("p h w -> p w h").unsqueeze(3).to_broadcast(
                                [64, 2, HP, HD]),
                            ALU.mult)
                    ins.then_inc(normed, 1)
                if i % 2 == 0 and has(i + 2):
                    h = (i + 2) // 2
                    v.wait_ge(qkt_done, h0 + (h + 1))
                    if h >= 2:
                        v.wait_ge(scores_done, p0 + (2 * h - 2))
                    for par in range(2):
                        v.tensor_scalar(q_hi[h % 2][:, :, par, :],
                                        qk_t[h % 2][:, 0, :].rearrange("p (w t) -> p w t", w=4),
                                        vec[:, EVEN + par:EVEN + par + 1], None, ALU.mult)
                    v.tensor_copy(k_hi[h % 2][:, :], qk_t[h % 2][:, 1, :]).then_inc(qk_hi_done, 1)
                if PAIRS - 4 <= i < PAIRS and followed:
                    for j in range(2):
                        stats(b + 1, 2 * (i - (PAIRS - 4)) + j)
                for t in low_in.get(i, ()):
                    low(b, t)

            def result(b, t):
                v.wait_ge(c2_done, b * T2N + (t + 1))
                v.scalar_tensor_tensor(yt[t % 2][:, :], c2_bank[t], c2_scale[:, 0:1],
                                       xr[:, T2R * t:T2R * (t + 1), :].rearrange("p i j -> p (i j)"),
                                       ALU.mult, ALU.add).then_inc(res_added, 1)
                v.wait_ge(res_added, b * T2N + (t + 1) + RES0)
                v.wait_ge(xf_biased, b * T2N + (t + 1))
                v.scalar_tensor_tensor(xf[t % NXF][:, :], yt[t % 2][:, :], x_down[:, 0:1], xf[t % NXF][:, :],
                                       ALU.mult, ALU.add).then_inc(y_ready, 1)

            def image(b, followed):
                steps(v, b, step, followed)
                if followed:
                    moments(b + 1)
                low(b, 9)
                border(b, BORDER1, 1)
                if followed:
                    scales(b + 1)
                    start_scales(b + 1)
                    row(0, (b + 1) * NROW)
                    row(1, (b + 1) * NROW)
                for t in range(BORDER1, T1N):
                    low(b, t)
                border(b, T1N, 2)
                for t in range(T2N - len(HEAD)):
                    result(b, t)
                if followed:
                    head(b + 1, step, result)
                else:
                    for t in range(T2N - len(HEAD), T2N):
                        result(b, t)

            for j in range(8):
                stats(0, j)
            moments(0)
            low_weights()
            scales(0, meanwhile=largest)
            qk_scales()
            row(0, 0)
            conv_scales()
            start_scales(0)
            row(1, 0)
            head(0, step)
            low_conv_weights()
            images(v, image)

        @block.gpsimd
        def _(pool):
            for t in v_bd:
                pool.memset(t[:, :, :, :], 0.0)
            for t in x_hi + x_lo:
                g = t[:, :, :].rearrange("p a (w i j) -> p a w i j", w=NWIN, i=TS)
                pool.memset(g[:, 0, :, 0:1, :], 0.0)
                pool.memset(g[:, 3, :, TS - 1:TS, :], 0.0)
            for t in (xr_hi, xr_lo):
                for k in (0, G + 1):
                    pool.memset(t[:, k:k + 1, :], 0.0)
                    ins = pool.memset(t[:, 1:G + 1, k:k + 1], 0.0)
            ins.then_inc(zeroed, 1)
            pool.wait_ge(zeroed, 1)
            for t in v_bd:
                pool.memset(t[0:64, :, 0, VW - 1:VW], 1.0)
                ins = pool.memset(t[64:128, :, 1, VW - 1:VW], 1.0)
            ins.then_inc(zeroed, 1)
            pool.wait_ge(zeroed, 2)
            pool.wait_ge(amax_done, 1)
            pool.partition_all_reduce(amax_all[:, 0:A_PROJ], amax[:, 0:A_PROJ], P, RMAX).then_inc(setup_pool, 1)
            pool.wait_ge(bias_scaled, 3)
            n = [0]

            def bias_link(ins):
                n[0] += 1
                ins.then_inc(bias_split, 1)
                pool.wait_ge(bias_split, n[0])

            for j in range(3):
                bias_link(pool.tensor_copy(b_tmp[:, :], bst[:, :]))
                bias_link(pool.tensor_copy(b_parts[32 * j:32 * j + 32, :], b_tmp[32 * j:32 * j + 32, :]))
                bias_link(pool.tensor_tensor(bst[:, :], bst[:, :], b_tmp[:, :], ALU.subtract))

            def begin(b, first):
                pool.wait_ge(gn_dve, b * 3 + 3)
                pool.tensor_tensor(gm[:, 4:5], gm[:, 3:4], neg_half[:, 0:1], ALU.pow).then_inc(gn_pool, 1)
                if first:
                    pool.wait_ge(amax_done, 2)
                    pool.partition_all_reduce(amax_all[:, A_PROJ:A_C2 + 1], amax[:, A_PROJ:A_C2 + 1], P, RMAX).then_inc(
                        setup_pool, 1)
                for r in range(2):
                    for a in range(4):
                        part(r, a, b * PAIRS, b * NROW, first)

            def part(r, a, p0, r0, first=False):
                pool.wait_ge(xhi_done, (r0 + r) * 4 + a + 1)
                if r >= 2 or not first:
                    pool.wait_ge(conv_done, p0 + (4 * r - 4))
                pool.tensor_tensor(at_offset(x_lo[r % 2], a), rows_under(xnf[r % 2], a),
                                   at_offset(x_hi[r % 2], a), ALU.subtract).then_inc(xlo_done, 1)

            def split(b, r):
                pool.wait_ge(xr_hi_done, b * NROW + (r + 1))
                rows = slice(TS * r + 1, TS * (r + 1) + 1)
                pool.tensor_tensor(xr_lo[:, rows, 1:G + 1], xr[:, TS * r:TS * (r + 1), :], xr_hi[:, rows, 1:G + 1],
                                   ALU.subtract).then_inc(xr_split, 1)

            def step(i, p0, h0, r0, rr0, row0, b=None, followed=False):
                if has(i + 4):
                    m = i + 4
                    j = m % 2
                    pool.wait_ge(ln_moments, p0 + (m + 1))
                    if m >= 2:
                        pool.wait_ge(ln_v, p0 + (m - 1))
                    pool.tensor_tensor(ln_ve[j][:, :], ln_mv[j][:, :, 1], eps_y[:, :], ALU.add)
                    pool.tensor_scalar(ln_nm[j][:, :], ln_mv[j][:, :, 0], -1.0, None, ALU.mult).then_inc(
                        ln_var_eps, 1)
                    pool.wait_ge(ln_var_eps, p0 + (m + 1))
                    pool.tensor_tensor(ln_rs[j][:, :], ln_ve[j][:, :], neg_half[:, 0:3], ALU.pow).then_inc(
                        ln_pow, 1)
                    pool.wait_ge(ln_pow, p0 + (m + 1))
                    pool.tensor_tensor(ln_nr[j][:, :], ln_nm[j][:, :], ln_rs[j][:, :], ALU.mult).then_inc(
                        ln_scales, 1)
                if has(i):
                    pool.wait_ge(maxed, p0 + (i + 1))
                    pool.tensor_tensor(sc[i % 4][:, :, :, :], sc[i % 4][:, :, :, :],
                                       mx[i % 2][:, :, :].unsqueeze(3).to_broadcast([P, HP, 2, TOK]),
                                       ALU.subtract).then_inc(shifted, 1)
                if 2 <= (i + 8) // 4 < NROW:
                    for a in ((0,), (1,), (2, 3), ())[i % 4]:
                        part((i + 8) // 4, a, p0, r0)
                for r in split_in.get(i, ()):
                    split(b, r)

            def image(b, followed):
                steps(pool, b, step, followed)
                split(b, NROW - 1)
                if followed:
                    begin(b + 1, False)
                    head(b + 1, step)

            begin(0, True)
            head(0, step)
            images(pool, image)

        @block.scalar
        def _(act):
            act.wait_ge(w_scaled, 1)
            for t in range(3):
                cols = slice(E * t, E * (t + 1))
                act.activation(w_hi[:, :, cols], wst[:, :, cols], ACT.Identity, scale=sw[:, t:t + 1]).then_inc(
                    w_hi_done, 1)
            act.wait_ge(zeroed, 2)

            def row(r, r0, rr0, first=False):
                act.wait_ge(loaded_xs[r % 2], (rr0 + (r // 2 + 1)) * 16)
                if not first:
                    act.wait_ge(xlo_done, (r0 + (r - 1)) * 4)
                act.activation(xnf[r % 2][:, :, :], xs[r % 2][:, :, :], ACT.Identity, scale=xn_aff[:, 0:1],
                               bias=xn_aff[:, 1:2]).then_inc(xn_raw, 1)

            def part(r, a, p0, r0, first=False):
                act.wait_ge(xn_done, r0 + (r + 1) + 1)
                if r >= 2 or not first:
                    act.wait_ge(conv_done, p0 + (4 * r - 4))
                act.activation(at_offset(x_hi[r % 2], a), rows_under(xnf[r % 2], a), ACT.Copy).then_inc(
                    xhi_done, 1)

            def gelu(b, t, src, **scaled):
                act.activation(hst[t % 6][:, :, :], src, ACT.Gelu, **scaled).then_inc(gelu_done, 1)

            def c1_tile(t):
                return c1_bank[t][:, 0:T1R * (G + 1)].rearrange("p (i j) -> p i j", i=T1R)

            def c1_out(b, t):
                act.wait_ge(c1_done, b * T1N + (t + 1))
                if t >= 6:
                    act.wait_ge(h_split, b * T1N + (t - 5))
                gelu(b, t, c1_tile(t), scale=y_down[:, 0:1], bias=vec[:, C1B:C1B + 1])

            def split(b, r):
                act.wait_ge(xr_added, b * NROW + (r + 1) + ADD0)
                act.activation(xr_hi[:, TS * r + 1:TS * (r + 1) + 1, 1:G + 1], xr[:, TS * r:TS * (r + 1), :],
                               ACT.Copy).then_inc(xr_hi_done, 1)

            def start_xr(k):
                act.activation(xr[:, G // 4 * k:G // 4 * (k + 1), :].rearrange("p i j -> p (i j)"),
                               xst[:, NT // 4 * k:NT // 4 * (k + 1)],
                               ACT.Identity, scale=gm[:, 7:8], bias=gm[:, 6:7]).then_inc(xr_begun, 1)

            def step(i, p0, h0, r0, rr0, row0, b=None, followed=False):
                if i % 4 == 3 and 2 <= (i + 9) // 4 < NROW:
                    row((i + 9) // 4, r0, rr0)
                if 2 <= (i + 8) // 4 < NROW:
                    for a in parts_of[i % 4]:
                        part((i + 8) // 4, a, p0, r0)
                if i % 2 == 0 and has(i + 2):
                    h = (i + 2) // 2
                    act.wait_ge(tr_done, p0 + (2 * h + 2))
                    if h >= 2:
                        act.wait_ge(qk_split, h0 + (h - 1))
                    for t in range(2):
                        ins = act.activation(qk_t[h % 2][:, t, :], t_ps[:, t, :, :].rearrange("p a n -> p (a n)"),
                                             ACT.Identity, scale=qk_aff[:, 2 * t:2 * t + 1],
                                             bias=qk_aff[:, 2 * t + 1:2 * t + 2])
                    ins.then_inc(qkt_done, 1)
                if has(i - 1):
                    m = i - 1
                    act.wait_ge(ptr_done, p0 + (m + 1))
                    if m >= 2:
                        act.wait_ge(pv_done, p0 + (m - 1))
                    act.activation(pt[m % 2][:, :, :], pt_ps[:, :, :], ACT.Copy).then_inc(pt_copied, 1)
                if i % 4 == 2 and i >= 6:
                    r = (i - 6) // 4
                    act.wait_ge(ot_done, p0 + (4 * r + 4))
                    if r >= 2:
                        act.wait_ge(proj_done, r0 + (r - 1))
                    for w in range(2):
                        for par in range(2):
                            ins = act.activation(
                                ot[r % 2][64 * par:64 * par + 64, :].rearrange("p (m w t) -> p m w t", w=2, t=TOK)[:, :, w, :],
                                ox_ps[64 * w:64 * w + 64, :].rearrange("p (m a t) -> p m a t", a=2, t=TOK)[:, :, par, :],
                                ACT.Copy)
                    ins.then_inc(ot_copied, 1)
                if has(i + 4):
                    m = i + 4
                    j = m % 2
                    act.wait_ge(ln_scales, p0 + (m + 1))
                    if m >= 2:
                        act.wait_ge(tr_done, p0 + (m - 1))
                    for t in range(2):
                        ins = act.activation(qk_n[j][:, t, :].rearrange("p (h y x) -> p h y x", h=HEADS, y=2),
                                             by_head(y_ps[j][:, E * t:E * (t + 1)]), ACT.Identity,
                                             scale=ln_rs[j][:, t:t + 1], bias=ln_nr[j][:, t:t + 1])
                    ins.then_inc(ln_qk, 1)
                    if m >= 8:
                        act.wait_ge(pv_done, p0 + (m - 7))
                    for w in range(2):
                        q = slice(64 * w, 64 * w + 64)
                        ins = act.activation(
                            v_bd[m % 8][q, :, w, 0:2 * HD].rearrange("p h (a y x) -> p h a y x", a=2, y=2),
                            y_ps[j][q, 2 * E:3 * E].rearrange("p (y h a x) -> p h a y x", y=2, h=HP, a=2),
                            ACT.Identity,
                            scale=ln_rs[j][q, 2:3], bias=ln_nr[j][q, 2:3])
                    ins.then_inc(ln_v, 1)
                if has(i):
                    act.wait_ge(shifted, p0 + (i + 1))
                    act.activation(sc[i % 4][:, :, :, :], sc[i % 4][:, :, :, :], ACT.Exp).then_inc(exped, 1)
                if i == PAIRS + 3:
                    split(b, NROW - 1)
                for t in c1_in.get(i, ()):
                    if t < RAW1:
                        act.wait_ge(c1_done, b * T1N + (t + 1))
                        act.activation(hst[t][:, :, :], c1_tile(t), ACT.Identity, scale=y_down[:, 0:1],
                                       bias=vec[:, C1B:C1B + 1]).then_inc(h_raw, 1)
                    else:
                        if t == RAW1:
                            act.wait_ge(h_raw, b * RAW1 + RAW1)
                            for u in range(RAW1):
                                gelu(b, u, hst[u][:, :, :])
                        c1_out(b, t)
                if i == 1:
                    act.wait_ge(res_added, b * T2N + RES0)
                    start_xr(3)
                for r in split_in.get(i, ()):
                    split(b, r)

            def bias(b, t):
                act.wait_ge(xf_loaded[t % NXF], (b * (T2N // NXF) + (t // NXF + 1)) * 16)
                act.activation(xf[t % NXF][:, :], xf[t % NXF][:, :], ACT.Identity, bias=vec[:, C2B:C2B + 1]).then_inc(
                    xf_biased, 1)

            def bias_and_start(b, t):
                bias(b, t)
                k = t - XR_FROM
                if 0 <= k < 3:
                    act.wait_ge(res_added, b * T2N + 2 * (k + 1) + RES0)
                    start_xr(k)

            def image(b, followed):
                steps(act, b, step, followed)
                for t in range(11, T1N):
                    c1_out(b, t)
                if followed:
                    act.wait_ge(xn_scales, b + 2)
                    for r in range(2):
                        row(r, (b + 1) * NROW, (b + 1) * (NROW // 2))
                for r in range(2):
                    if followed:
                        for a in range(4):
                            part(r, a, (b + 1) * PAIRS, (b + 1) * NROW)
                    for t in (2 * r, 2 * r + 1):
                        bias(b, t)
                act.activation(wait_exp[:, :], vec[:, 0:1], ACT.Exp)
                if followed:
                    head(b + 1, step, bias_and_start, tile_first=True)
                else:
                    for t in range(T2N - len(HEAD), T2N):
                        bias(b, t)

            act.wait_ge(xn_scales, 1)
            for r in range(2):
                row(r, 0, 0, first=True)
            for r in range(2):
                for a in range(4):
                    part(r, a, 0, 0, first=True)
            act.activation(wait_exp[:, :], vec[:, 0:1], ACT.Exp)
            act.wait_ge(c_scales, 1)
            for j, (w, hi) in enumerate(((w1s, w1_hi), (w2s, w2_hi))):
                act.activation(hi[:, :, :], w[:, :, :], ACT.Identity, scale=w_up[:, j:j + 1]).then_inc(c_hi_done, 1)
            act.wait_ge(gn_chain, 7)
            head(0, step, lambda b, t: start_xr(t - XR_FROM) if t >= XR_FROM else None)
            images(act, image)

        @block.tensor
        def _(pe):
            pe.wait_ge(loaded_consts, 16 * 6)
            pe.matmul(pt_ps[:, 0, 0:1], projw[:, :], vec[:, BV:BV + 1], start=True, stop=True).then_inc(setup_pe, 1)
            def mean_of_phases(b, n, of):
                pe.wait_ge(gn_dve, b * 3 + n)
                pe.matmul(ox_ps[:, 0:1], selm[:, :], of, start=True, stop=True).then_inc(gn_pe, 1)

            def c1(b, t):
                if t == 0:
                    pe.wait_ge(c_scaled, 2)
                pe.wait_ge(xr_split, b * NROW + min((T1R * (t + 1) - 1) // TS, NROW - 1) + 1)
                if t < 2:
                    pe.wait_ge(ln_v, b * PAIRS + PAIRS - 1 + t)
                elif t < RAW1:
                    pe.wait_ge(h_raw, b * RAW1 + (t - 1))
                elif t < 6:
                    pe.wait_ge(biased, b * PAIRS + PAIRS)
                elif t < 8:
                    pe.wait_ge(h_raw, b * RAW1 + (t - 3))
                else:
                    pe.wait_ge(gelu_done, b * T1N + (t - 3))
                for a in range(4):
                    ay, ax = a // 2, a % 2
                    for n, (ww, xx) in enumerate(((w1_hi, xr_hi), (w1_hi, xr_lo), (w1_lo, xr_hi))):
                        ins = pe.matmul(c1_bank[t][:, 0:T1R * (G + 1)], ww[:, a, :],
                                        xx[:, T1R * t + ay:T1R * (t + 1) + ay, ax:ax + G + 1],
                                        start=(a == 0 and n == 0), stop=(a == 3 and n == 2))
                ins.then_inc(c1_done, 1)

            def by_feature(m, p0, r0):
                if has(m):
                    pe.wait_ge(normed, p0 + (m + 1))
                    if m % 4 == 0:
                        pe.wait_ge(xr_added, r0 + m // 4 + ADD0)
                    pe.transpose(ox_ps[:, P * (m % 4):P * (m % 4 + 1)], on[m % 2][:, :, :, :].rearrange(
                        "p w h d -> p (w h d)"), idf[:, :]).then_inc(ot_done, 1)

            def step(i, p0, h0, r0, rr0, row0, b=None, followed=False):
                if has(i + 4):
                    m = i + 4
                    r, s = m // 4, m % 4
                    if s == 0:
                        pe.wait_ge(xlo_done, (r0 + (r + 1)) * 4)
                    if m >= 2:
                        pe.wait_ge(ln_v, p0 + (m - 1))
                    y = y_ps[m % 2][:, 0:QKV]
                    pe.matmul(y, ones_b[0:96, :], b_parts[0:96, :], start=True, stop=False)
                    for a in range(4):
                        cols = {0: slice(0, E // 2), 3: slice(E // 2, E)}.get(a, slice(0, E))
                        for xx, ww in ((x_hi, w_hi), (x_hi, w_lo), (x_lo, w_hi)):
                            ins = pe.matmul(y.rearrange("p (t e) -> p t e", t=3)[:, :, cols],
                                            xx[r % 2][:, a, P * s:P * (s + 1)],
                                            ww[:, a, :].rearrange("p (t e) -> p t e", t=3)[:, :, cols],
                                            start=False, stop=(a == 3 and xx is x_lo))
                    ins.then_inc(conv_done, 1)
                if i < PAIRS + 3:
                    for t in c1_in.get(i, ()):
                        c1(b, t)
                if i == PAIRS + 3:
                    c1(b, c1_in[i][0])
                if i % 4 == 3 and i >= 7:
                    r = (i - 7) // 4
                    pe.wait_ge(ot_copied, r0 + (r + 1))
                    pe.matmul(ox_ps[:, :], projg[:, :], ot[r % 2][:, :], start=True, stop=True).then_inc(
                        proj_done, 1)
                if has(i + 3):
                    m = i + 3
                    pe.wait_ge(ln_qk, p0 + (m + 1))
                    if m % 2 == 0 and m >= 2:
                        pe.wait_ge(qkt_done, h0 + m // 2)
                    for t in range(2):
                        ins = pe.transpose(t_ps[:, t, m % 2, :], qk_n[m % 2][:, t, :], idf[:, :])
                    ins.then_inc(tr_done, 1)
                if i % 4 == 0:
                    by_feature(i - 4, p0, r0)
                if i == PAIRS + 3:
                    for t in c1_in[i][1:]:
                        c1(b, t)
                if has(i):
                    h = i // 2
                    pe.wait_ge(qk_split, h0 + (h + 1))
                    if i == 0:
                        pe.wait_ge(res_added, b * T2N + RES0)
                    if i >= 1:
                        pe.wait_ge(biased, p0 + i)
                    for hp in range(HP):
                        rows = slice(32 * hp, 32 * hp + 32)
                        if hp >= 2:
                            pe.wait_ge(scores_bank, (p0 + i) * 2 + (hp - 1))
                        for w in range(2):
                            tok = slice(P * (i % 2) + TOK * w, P * (i % 2) + TOK * (w + 1))
                            c0 = (hp // 2) * 128 + TOK * w
                            for n, (qq, kk) in enumerate(((q_hi, k_hi), (q_hi, k_lo), (q_lo, k_hi))):
                                ins = pe.matmul(s_ps[:, hp % 2, c0:c0 + TOK],
                                                qq[h % 2][rows, 2 * (i % 2) + w, :, :].rearrange("p a t -> p (a t)"),
                                                kk[h % 2][rows, tok], start=(n == 0), stop=(n == 2))
                        if hp < 2:
                            ins.then_inc(scores_bank, 1)
                    ins.then_inc(scores_done, 1)
                if has(i - 1):
                    m = i - 1
                    pe.wait_ge(exped, p0 + (m + 1))
                    if m >= 1:
                        pe.wait_ge(pt_copied, p0 + m)
                    for g in range(HP):
                        ins = pe.transpose(pt_ps[:, g, :], sc[m % 4][:, g, :, :].rearrange("p w k -> p (w k)"),
                                           idf[:, :])
                    ins.then_inc(ptr_done, 1)
                if has(i - 2):
                    m = i - 2
                    pe.wait_ge(pt_copied, p0 + (m + 1))
                    if m >= 1:
                        pe.wait_ge(normed, p0 + m)
                    for g in range(HP):
                        ins = pe.matmul(o_ps[:, g, :, :].rearrange("p w d -> p (w d)"), pt[m % 2][:, g, :],
                                        v_bd[m % 8][:, g, :, :].rearrange("p w d -> p (w d)"),
                                        start=True, stop=True)
                    ins.then_inc(pv_done, 1)
                if i % 4 != 3:
                    by_feature(i - 3, p0, r0)

            def c2(b, t):
                if t == 0:
                    pe.wait_ge(h_border, b * 2 + 1)
                if T2R * (t + 1) + 1 > T1R * BORDER1:
                    pe.wait_ge(h_border, b * 2 + 2)
                if 1 <= t < 4:
                    pe.wait_ge(gelu_done, b * T1N + (10 + t))
                elif t >= 4:
                    pe.wait_ge(res_added, b * T2N + (3, 4, 5, 6)[t - 4] + RES0)
                for a in range(4):
                    ay, ax = a // 2, a % 2
                    for n, (ww, hh) in enumerate(((w2_hi, h_hi), (w2_hi, h_lo), (w2_lo, h_hi))):
                        ins = pe.matmul(c2_bank[t], ww[:, a, :],
                                        hh[:, T2R * t + ay:T2R * (t + 1) + ay, ax:ax + G],
                                        start=(a == 0 and n == 0), stop=(a == 3 and n == 2))
                ins.then_inc(c2_done, 1)

            def image(b, followed):
                steps(pe, b, step, followed)
                c1(b, 11)
                if followed:
                    mean_of_phases(b + 1, 1, gmv[:, 0:1])
                c1(b, 12)
                if followed:
                    mean_of_phases(b + 1, 2, gm[:, 2:3])
                for t in range(T2N - len(HEAD)):
                    c2(b, t)
                if followed:
                    pe.wait_ge(res_added, b * T2N + 2 + RES0)
                    head(b + 1, step, c2)
                else:
                    for t in range(T2N - len(HEAD), T2N):
                        c2(b, t)

            mean_of_phases(0, 1, gmv[:, 0:1])
            mean_of_phases(0, 2, gm[:, 2:3])
            pe.wait_ge(weights_ready, 3)
            pe.wait_ge(bias_split, 9)
            pe.wait_ge(zeroed, 2)
            head(0, step)
            pe.wait_ge(c_scales, 1)
            images(pe, image)


def _phases(n):
    p = np.arange(P)
    return p // (2 * C), p // C % 2, p % C


def _group_weights(w, e_out, shift):
    py, px, ci = _phases(P)
    oy, ox, co = e_out
    wp = np.zeros((P, 4, len(co)), w.dtype)
    for a in range(4):
        ky = (2 * (a // 2) + shift[0] * py[:, None] + shift[1] * oy[None, :] + shift[2]) + 0 * co[None, :]
        kx = (2 * (a % 2) + shift[0] * px[:, None] + shift[1] * ox[None, :] + shift[2]) + 0 * co[None, :]
        ok = (ky >= 0) & (ky < 3) & (kx >= 0) & (kx < 3)
        k, m = np.nonzero(ok)
        wp[k, a, m] = w[co[m], ci[k], ky[k, m], kx[k, m]]
    return wp


def _row_weights(w, e_out):
    col, ci = np.divmod(np.arange(P), C)
    oy, ox, co = e_out
    wp = np.zeros((P, 4, len(co)), w.dtype)
    for a in range(4):
        ky = a - oy[None, :] + 0 * ci[:, None]
        kx = col[:, None] - ox[None, :]
        k, m = np.nonzero((ky >= 0) & (ky < 3) & (kx >= 0) & (kx < 3))
        wp[k, a, m] = w[co[m], ci[k], ky[k, m], kx[k, m]]
    return wp


def kernel(**inputs):
    import concourse.bacc as _bacc
    from concourse.bass_utils import run_bass_kernel_spmd as _run

    arrays, outputs = _lay_out(inputs)
    nc = _bacc.Bacc("TRN2", target_bir_lowering=False, num_devices=1)
    args = {n: nc.dram_tensor(f"in_{n}_dram", a.shape, mybir.dt.from_np(a.dtype), kind="ExternalInput").ap()
            for n, a in arrays.items()}
    out = nc.dram_tensor("out_0_dram", (B, P, NT), F32, kind="ExternalOutput").ap()
    conv_attention(nc, out=out, **args)
    r = _run(nc, [{f"in_{n}_dram": a for n, a in arrays.items()}], core_ids=[0])
    y = r.results[0]["out_0_dram"].reshape(B, 2, 2, C, G, G)
    return np.ascontiguousarray(y.transpose(0, 3, 4, 1, 5, 2)).reshape(B, C, IMG, IMG)


def _lay_out(inputs):
    g = {k.replace("L0_conv_", ""): np.asarray(v) for k, v in inputs.items()}
    x = g["x"]
    xp = x.reshape(B, C, G, 2, G, 2).transpose(0, 3, 5, 1, 2, 4)
    x_al = np.ascontiguousarray(xp).reshape(B, P, NT)
    win = np.zeros((B, C, NROW, NWIN, HROWS, HROWS), x.dtype)
    win[..., 1:-1, 1:-1] = x.reshape(B, C, NROW, WIN, NWIN, WIN).transpose(0, 1, 2, 4, 3, 5)
    x_sh = np.stack([win[..., c:c + 2 * TS:2] for c in range(4)], axis=1).reshape(B, P, NROW, NWIN * HWIN)

    e = np.arange(E)
    order = [hp for bank in range(2) for hp in range(bank, HP, 2)]
    hd, py, c4, px = np.unravel_index(e, (HEADS, 2, HD // 4, 2))
    f_nat = (hd * (HD // 4) + c4) * 4 + py * 2 + px
    py, hd, c4, px = np.unravel_index(e, (2, HEADS, HD // 4, 2))
    e_qk = (py, px, hd * (HD // 4) + c4)
    hd_v = 2 * np.array(order)[hd // 2] + hd % 2
    e_v = (py, px, hd_v * (HD // 4) + c4)
    r_v = np.concatenate([f_nat[HD * (2 * hp + par):HD * (2 * hp + par + 1)] for par in range(2) for hp in order])
    e_ph = _phases(P)
    e_m = e_ph[2] * 4 + e_ph[0] * 2 + e_ph[1]
    wqkv = np.concatenate([_row_weights(g["qw"], e_qk), _row_weights(g["kw"], e_qk), _row_weights(g["vw"], e_v)],
                          axis=2)
    bqkv = np.concatenate([g["qb"][e_qk[2]], g["kb"][e_qk[2]], g["vb"][e_v[2]]])
    bqkv = np.ascontiguousarray(np.broadcast_to(bqkv, (P, QKV)))
    w1 = _group_weights(g["c1w"], e_ph, (1, 1, -1))
    w2 = _group_weights(g["c2w"], e_ph, (-1, -1, 1))
    pos = np.stack(np.meshgrid(np.arange(TS), np.arange(TS), indexing="ij")).reshape(2, -1)
    rel = pos[:, :, None] - pos[:, None, :] + TS - 1
    full = g["bias_table"][rel[0] * (2 * TS - 1) + rel[1]]
    bias_t = np.stack([full[:, :, [2 * hp + par for hp in order]] for par in range(2)])
    bias_t = np.broadcast_to(bias_t.transpose(0, 1, 3, 2)[:, :, :, None, :], (2, TOK, HP, 2, TOK))
    bias_t = np.ascontiguousarray(bias_t).reshape(P, 2, HP * TOK)
    proj_t = np.ascontiguousarray(g["proj_w"][e_m][:, r_v].T)
    even = (e // HD % 2 == 0).astype(np.float32)
    vecs = np.stack([g["gq"][f_nat], g["bq"][f_nat], g["gk"][f_nat], g["bk"][f_nat], g["gv"][r_v], g["bv"][r_v],
                     g["proj_b"][e_m], g["c1b"][e_ph[2]], even, 1 - even, g["c2b"][e_ph[2]]], axis=1)
    ident = np.eye(P, dtype=np.float32)
    sel_mean = (e[:, None] % C == e[None, :] % C).astype(np.float32) / 4
    sel_ones = np.zeros((P, P), np.float32)
    sel_ones[[0, 32, 64]] = 1.0
    arrays = dict(x_al=x_al, x_sh=x_sh, wqkv=wqkv, bqkv=bqkv, bias_t=bias_t, proj_t=proj_t, vecs=vecs,
                  w1=w1, w2=w2, ident=ident, sel_mean=sel_mean, sel_ones=sel_ones)
    return {k: np.ascontiguousarray(v) for k, v in arrays.items()}, None
```
